# Optimizing a Trainium2 kernel written in Bass

```python
import numpy as np
import jax
import jax.numpy as jnp

def _softmax(x, axis=-1):
    return jax.nn.softmax(x, axis=axis)

def _gelu(x):
    return jax.nn.gelu(x, approximate=True)

def _silu(x):
    return jax.nn.silu(x)

def _sigmoid(x):
    return jax.nn.sigmoid(x)

def _layernorm(x, axis=-1, eps=1e-05):
    m = jnp.mean(x, axis=axis, keepdims=True)
    v = jnp.var(x, axis=axis, keepdims=True)
    return (x - m) / jnp.sqrt(v + eps)

def _scatter_add(tgt, idx, src, axis=0):
    return tgt.at[idx].add(src)

def _segment_sum(src, seg, n):
    return jax.ops.segment_sum(src, seg, n)
kernel_name = 'mk_adj_resnorm_d2_adj_r2_73db6b'

def setup_inputs(seed: int=0):
    np.random.seed(seed)
    _w = jnp.asarray

    def _rec_inputs():
        import jax
        import jax.numpy as jnp
        _gk = jax.random.key(seed)
        x = 7.22e-05 + 1 * jax.random.normal(jax.random.fold_in(_gk, 1), (8, 1024, 256), jnp.float32)
        _w = (1.0 + jnp.arange(1024, dtype=jnp.float32)) ** (-0.5)
        _w = _w / _w.mean()
        _pij = jnp.clip(0.015625 * _w[:, None] * _w[None, :], 0.0, 1.0)
        _a = jax.random.uniform(jax.random.fold_in(_gk, 2), (1024, 1024)) < _pij
        _af = _a.astype(jnp.float32)
        adj = _af
        return (x, adj)
    x, adj = _rec_inputs()

    def _L0_gnn_setup():
        import jax, jax.numpy as jnp
        import numpy as np
        B, N, D = (8, 1024, 256)
        key = jax.random.key(seed)
        k1, k2, k3, k4, k5 = jax.random.split(key, 5)
        neuron_states = jax.random.normal(k1, (B, N, D), dtype=jnp.float32)
        adjacency = jax.random.randint(k2, (N, N), 0, 2).astype(jnp.float32)
        scale = 1.0 / np.sqrt(D)
        Wq = jax.random.normal(k3, (D, D), dtype=jnp.float32) * scale
        Wk = jax.random.normal(k4, (D, D), dtype=jnp.float32) * scale
        Wv = jax.random.normal(k5, (D, D), dtype=jnp.float32) * scale
        return {'neuron_states': neuron_states, 'adjacency': adjacency, 'Wq': Wq, 'Wk': Wk, 'Wv': Wv}
    _L0_gnn_all = _L0_gnn_setup()
    _L0_gnn_in = {k: v for k, v in _L0_gnn_all.items() if k in ('Wq', 'Wk', 'Wv')}
    del _L0_gnn_all

    def _L1_gnn_setup():
        import jax, jax.numpy as jnp
        import numpy as np
        B, N, D, H = (4, 1024, 256, 8)
        HD = D // H
        key = jax.random.key(seed)
        ks = jax.random.split(key, 10)
        x = jax.random.normal(ks[0], (B, N, D), dtype=jnp.float32)
        adj = (jax.random.uniform(ks[1], (N, N)) < 0.1).astype(jnp.float32)
        s = 1.0 / np.sqrt(D)
        Wq = jax.random.normal(ks[2], (D, D), dtype=jnp.float32) * s
        Wk = jax.random.normal(ks[3], (D, D), dtype=jnp.float32) * s
        Wv = jax.random.normal(ks[4], (D, D), dtype=jnp.float32) * s
        Wo = jax.random.normal(ks[5], (D, D), dtype=jnp.float32) * s
        bq = jnp.zeros((D,), jnp.float32)
        bk = jnp.zeros((D,), jnp.float32)
        bv = jnp.zeros((D,), jnp.float32)
        bo = jnp.zeros((D,), jnp.float32)
        return {'x': x, 'adj': adj, 'Wq': Wq, 'bq': bq, 'Wk': Wk, 'bk': bk, 'Wv': Wv, 'bv': bv, 'Wo': Wo, 'bo': bo}
    _L1_gnn_all = _L1_gnn_setup()
    _L1_gnn_in = {k: v for k, v in _L1_gnn_all.items() if k in ('Wq', 'bq', 'Wk', 'bk', 'Wv', 'bv', 'Wo', 'bo')}
    del _L1_gnn_all
    return {'x': x, 'adj': adj, 'L0_gnn_Wq': _L0_gnn_in['Wq'], 'L0_gnn_Wk': _L0_gnn_in['Wk'], 'L0_gnn_Wv': _L0_gnn_in['Wv'], 'L1_gnn_Wq': _L1_gnn_in['Wq'], 'L1_gnn_bq': _L1_gnn_in['bq'], 'L1_gnn_Wk': _L1_gnn_in['Wk'], 'L1_gnn_bk': _L1_gnn_in['bk'], 'L1_gnn_Wv': _L1_gnn_in['Wv'], 'L1_gnn_bv': _L1_gnn_in['bv'], 'L1_gnn_Wo': _L1_gnn_in['Wo'], 'L1_gnn_bo': _L1_gnn_in['bo']}

def reference(x, adj, L0_gnn_Wq, L0_gnn_Wk, L0_gnn_Wv, L1_gnn_Wq, L1_gnn_bq, L1_gnn_Wk, L1_gnn_bk, L1_gnn_Wv, L1_gnn_bv, L1_gnn_Wo, L1_gnn_bo):
    import jax
    import jax.numpy as jnp

    def _L0_gnn_ref(neuron_states, adjacency, Wq, Wk, Wv):
        import jax, jax.numpy as jnp
        import numpy as np
        B, N, D = (8, 1024, 256)
        q = jnp.einsum('bnd,ed->bne', neuron_states, Wq)
        k = jnp.einsum('bnd,ed->bne', neuron_states, Wk)
        v = jnp.einsum('bnd,ed->bne', neuron_states, Wv)
        rel = jnp.einsum('bnd,bmd->bnm', q, k)
        rel = adjacency.T[None, :, :] * rel
        rel = rel / jnp.linalg.norm(rel, axis=2, keepdims=True)
        return jnp.einsum('bnm,bmd->bnd', rel, v)

    def _L1_gnn_ref(x, adj, Wq, bq, Wk, bk, Wv, bv, Wo, bo):
        import jax, jax.numpy as jnp
        import numpy as np
        B, N, D, H = (4, 1024, 256, 8)
        HD = D // H
        b, n, d = x.shape
        q = (x @ Wq + bq).reshape(b, n, H, HD)
        k = (x @ Wk + bk).reshape(b, n, H, HD)
        v = (x @ Wv + bv).reshape(b, n, H, HD)
        scores = jnp.einsum('bqhd,bkhd->bhqk', q, k) / jnp.sqrt(jnp.float32(HD))
        scores = scores + (1.0 - adj)[None, None, :, :] * -1000000000.0
        attn = jax.nn.softmax(scores, axis=-1)
        out = jnp.einsum('bhqk,bkhd->bqhd', attn, v).reshape(b, n, d)
        return out @ Wo + bo
    x = _layernorm(x + _L0_gnn_ref(x, adj, L0_gnn_Wq, L0_gnn_Wk, L0_gnn_Wv), axis=-1)
    x = _layernorm(x + _L1_gnn_ref(x, adj, L1_gnn_Wq, L1_gnn_bq, L1_gnn_Wk, L1_gnn_bk, L1_gnn_Wv, L1_gnn_bv, L1_gnn_Wo, L1_gnn_bo), axis=-1)
    return x

_drawn_inputs = setup_inputs


def setup_inputs(seed=0):
    import zlib

    import numpy as np

    out = dict(_drawn_inputs(seed))
    spreads = {'L1_gnn_bq': (0.0, 0.1),
     'L1_gnn_bk': (0.0, 0.1),
     'L1_gnn_bv': (0.0, 0.1),
     'L1_gnn_bo': (0.0, 0.1)}
    factors = {}
    for name, (base, spread) in spreads.items():
        noise = np.random.default_rng([zlib.crc32(name.encode()), seed]).standard_normal(out[name].shape)
        drawn = base * np.exp(spread * noise) if base else spread * noise
        out[name] = jnp.asarray(drawn.astype(out[name].dtype))
    for name, factor in factors.items():
        out[name] = (out[name] * factor).astype(out[name].dtype)
    return out
```

```python
from contextlib import ExitStack

import numpy as np

import concourse.bass as bass
from concourse import mybir

ALU = mybir.AluOpType
ACT = mybir.ActivationFunctionType
F32 = mybir.dt.float32
F32R = mybir.dt.float32r

B, N, D, H = 8, 1024, 256, 8
HD = D // H
P = 128
C = D // P
T = N // P
HALF = 512
TH = HALF // P
HPG = P // HD
HG = H // HPG
GQ = 256
QT = GQ // P
UPG = QT * HPG
GROUPS = HG * (N // GQ)
UNITS = GROUPS * UPG
MASK = 1.0e9
EPS = 1e-5
QSCALE = -1.0 / float(np.sqrt(np.float32(HD)))
RING = 6
SUMS, COLS = 6, 7
NRING = 3
ADJ = 4


def job_list():
    jobs = [(("xT", c, q), "act" if (c + q) % 2 else "dve") for c in range(C) for q in range(2)]
    jobs += [(("G", m, h), "act" if (m + h) % 2 else "dve") for m in range(C) for h in range(2)]
    jobs += [(("v0", p), "act" if p % 2 else "dve") for p in range(T // 2)]
    jobs += [(("rel", 0, m), "dve") for m in range(T)]
    jobs += [(("out", 0, t), "dve") for t in range(TH)]
    jobs += [(("rel", 1, m), "dve") for m in range(T)]
    jobs += [(("x1T", 0, c), "act") for c in range(C)]
    jobs += [(("qk", 0, w), "act") for w in range(2 * HG)]
    jobs += [(("out", 1, t), "dve") for t in range(TH)]
    jobs += [(("v1", 0, p), "dve") for p in range(TH // 2)]
    jobs += [(("x1T", 1, c), "act") for c in range(C)]
    jobs += [(("qk", 1, w), "act") for w in range(2 * HG)]
    jobs += [(("v1", 1, p), "dve") for p in range(TH // 2)]
    jobs += [(("wo", p), "dve") for p in range(T // 2)]
    return jobs


JOBS = job_list()
INDEX = {name: i for i, (name, _) in enumerate(JOBS)}
DRAINS = {e: sum(1 for _, x in JOBS if x == e) for e in ("act", "dve")}


def bank(name):
    return INDEX[name] % RING


def filled(name):
    return INDEX[name] + 1


def drained(name):
    i = INDEX[name]
    e = JOBS[i][1]
    return e, sum(1 for _, x in JOBS[:i + 1] if x == e)


def unit(u):
    g, r = divmod(u, UPG)
    hg, qp = divmod(g, N // GQ)
    qi, j = divmod(r, HPG)
    return g, hg, qp * GQ, qi, j


def build(nc, x, adj, wq0, wk0, wv0, wq1, bq1, wk1, bk1, wv1, bv1, wo1, bo1, out):
    with ExitStack() as ctx:
        def sb(name, shape, dt=F32):
            return ctx.enter_context(nc.sbuf_tensor(name, shape, dt))

        def sem(name):
            return ctx.enter_context(nc.semaphore(name))

        PS = ctx.enter_context(nc.psum_tensor("PS", [P, 8, HALF], F32))

        negmask = sb("negmask", [P, T, N])
        A0 = sb("A0", [P, C, D])
        wv0T = sb("wv0T", [P, C, D])
        wq = sb("wq", [P, C, D])
        wk = sb("wk", [P, C, D])
        wv = sb("wv", [P, C, D])
        wo = sb("wo", [P, C, D])
        bqc = sb("bqc", [P, C])
        bkc = sb("bkc", [P, C])
        bvb = sb("bvb", [P, D])
        bob = sb("bob", [P, D])
        ident = sb("ident", [P, P])
        ones = sb("ones", [P, HD])
        pick = sb("pick", [P, 1])
        mhalf = sb("mhalf", [P, T])
        eps = sb("eps", [P, T])
        xs = sb("xs", [P, T, D])
        x1 = sb("x1", [P, T, D])
        vs = sb("vs", [P, T, D])
        QO = sb("QO", [P, HG, N])
        qlo = sb("qlo", [P, HG, N])
        KS = sb("KS", [P, H, N])
        QS = sb("QS", [P, 2, HPG, GQ])
        nr = sb("nr", [P, NRING, N])
        pt = sb("pt", [P, 2, HPG, T, GQ])
        qhi = QO
        v0 = nr[:, 0:2, :].rearrange("p a n -> p (a n)").rearrange("p (t d) -> p t d", d=D)
        lower = pt[:, 0].rearrange("p j t q -> p (j t q)")
        upper = pt[:, 1].rearrange("p j t q -> p (j t q)")

        def part(flat, k, n):
            return flat[:, k * N:(k + n) * N]

        relm = [part(upper, 0, 4).rearrange("p (m n) -> p m n", n=HALF),
                part(upper, 4, 4).rearrange("p (m n) -> p m n", n=HALF)]
        khi = part(upper, 0, 2).rearrange("p (g n) -> p g n", n=N)
        klo = part(upper, 2, 2).rearrange("p (g n) -> p g n", n=N)
        xT = part(lower, 0, 2).rearrange("p (c n) -> p c n", c=C)
        GT = part(lower, 2, 2).rearrange("p (c n) -> p c n", c=C)
        x1T = GT
        sq = part(lower, 4, 2).rearrange("p (k n) -> p k n", n=HALF)
        adjr = part(lower, 6, 2).rearrange("p (k n) -> p k n", n=HALF)
        qf = sq[:, 0:2]
        sums = nr[:, 2, 0:HALF]
        nsq = sb("nsq", [P, T])
        rnorm = sb("rnorm", [P, T])
        stats = sb("stats", [P, T, 6])
        mv = sb("mv", [P, T, 2])
        rstd = sb("rstd", [P, T])
        least = sb("least", [P, UNITS])
        rowsum = sb("rowsum", [P, UNITS])
        rrow = sb("rrow", [P, UPG])
        rexp = sb("rexp", [P, QT, HPG, HD])
        rT = sb("rT", [P, GQ])

        passed = sem("passed")
        w_in = sem("w_in")
        consts = sem("consts")
        setup_pe = sem("setup_pe")
        setup_dve = sem("setup_dve")
        mask_ready = sem("mask_ready")
        x_in = sem("x_in")
        adj_in = [sem(f"adj_in{k}") for k in range(ADJ)]
        bank_filled = sem("bank_filled")
        act_drained = sem("act_drained")
        dve_drained = sem("dve_drained")
        squared = sem("squared")
        sums_added = sem("sums_added")
        sums_out = sem("sums_out")
        cols_ready = sem("cols_ready")
        nsq_ready = sem("nsq_ready")
        rnorm_ready = sem("rnorm_ready")
        stat_step = sem("stat_step")
        var_ready = sem("var_ready")
        pool_step = sem("pool_step")
        rstd_ready = sem("rstd_ready")
        x1_ready = sem("x1_ready")
        x1b_ready = sem("x1b_ready")
        qf_ready = sem("qf_ready")
        hi_ready = sem("hi_ready")
        lo_ready = sem("lo_ready")
        ks_in = [sem(f"ks_in{g}") for g in range(HG)]
        qs_in = [sem(f"qs_in{g}") for g in range(2)]
        scores = sem("scores")
        masked = sem("masked")
        probs = sem("probs")
        turned_a = sem("turned_a")
        turned_b = sem("turned_b")
        pt_a = sem("pt_a")
        pt_b = sem("pt_b")
        rrow_ready = sem("rrow_ready")
        rexp_ready = sem("rexp_ready")
        rT_filled = sem("rT_filled")
        rT_ready = sem("rT_ready")
        pv_done = sem("pv_done")
        o_ready = sem("o_ready")
        y_ready = sem("y_ready")
        out_done = sem("out_done")

        block = ctx.enter_context(nc.Block())
        xv = x.rearrange("b (t p) d -> b p t d", p=P)
        ov = out.rearrange("b (t p) d -> b p t d", p=P)
        adjv = adj.rearrange("(t p) n -> p t n", p=P)
        wview = lambda w: w.rearrange("(c p) e -> p c e", p=P)
        w0 = part(lower, 0, 2).rearrange("p (w c d) -> p w c d", w=4, c=C)
        row = lambda v: v.rearrange("(a n) -> a n", a=1)
        QUARTER = 4

        def alone(eng, signal, value):
            eng.wait_ge(signal, value)
            eng.sem_inc(passed, 1)

        def load_q(sp, g):
            _, hg, q0, _, _ = unit(g * UPG)
            for j in range(HPG):
                for r, src in enumerate((qhi, qhi, qlo, qlo)):
                    sp.dma_start(QS[r * HD:(r + 1) * HD, g % 2, j, :],
                                 src[j * HD:(j + 1) * HD, hg, q0:q0 + GQ]).then_inc(qs_in[g % 2], 16)

        def inverse_deviation(pool, b, k, tiles, steps):
            pool.wait_ge(var_ready, b * 3 + k + 1)
            pool.tensor_tensor(rstd[:, tiles], mv[:, tiles, 1], eps[:, tiles], ALU.add).then_inc(pool_step, 1)
            pool.wait_ge(pool_step, steps + 1)
            pool.tensor_tensor(rstd[:, tiles], rstd[:, tiles], mhalf[:, tiles], ALU.pow).then_inc(rstd_ready, 1)

        def rowsums_out(act, b, g):
            act.wait_ge(rT_filled, b * GROUPS + g + 1)
            act.wait_ge(o_ready, 1 + b * GROUPS + g)
            act.activation(rT[:], PS[:, COLS, 0:GQ], ACT.Copy).then_inc(rT_ready, 1)

        @block.sync
        def _(sp):
            for w, src in enumerate((wq0, wk0, wv0)):
                sp.dma_start(w0[:, w], wview(src)).then_inc(w_in, 16)
            for dst, src in ((wq, wq1), (wk, wk1), (wv, wv1), (wo, wo1)):
                sp.dma_start(dst[:], wview(src)).then_inc(w_in, 16)
            for dst, src in ((bvb, bv1), (bob, bo1)):
                sp.dma_start(dst[:], row(src).to_broadcast([P, D])).then_inc(w_in, 16)
            for dst, src in ((bqc, bq1), (bkc, bk1)):
                for c in range(C):
                    sp.dma_start(dst[:, c:c + 1], src[c * P:(c + 1) * P].rearrange("(p a) -> p a", a=1)) \
                      .then_inc(w_in, 16)
            sp.dma_start(negmask[:], adjv).then_inc(w_in, 16)
            with sp.Fori(0, B) as b:
                alone(sp, x1_ready, 1 + b * T)
                sp.dma_start(xs[:], xv[bass.ds(b, 1)].rearrange("o p t d -> p (o t) d")).then_inc(x_in, 16)
                for h in range(2):
                    for m in range(T):
                        i = h * T + m
                        if i < ADJ:
                            sp.wait_ge(pv_done, 1 + b * GROUPS)
                        else:
                            h0, m0 = divmod(i - ADJ, T)
                            sp.wait_ge(dve_drained, 1 + b * DRAINS["dve"] + drained(("rel", h0, m0))[1])
                        sp.dma_start(adjr[:, i % ADJ], adjv[:, m, h * HALF:(h + 1) * HALF]) \
                          .then_inc(adj_in[i % ADJ], 16)
                for h in range(2):
                    cols = slice(h * HALF, (h + 1) * HALF)
                    for hg in range(HG):
                        sp.wait_ge(lo_ready, b * 4 * HG + (h * HG + hg + 1) * 2)
                        for j in range(HPG):
                            for g, src in enumerate((khi, klo, khi, klo)):
                                sp.dma_start(KS[g * HD:(g + 1) * HD, hg * HPG + j, cols],
                                             src[j * HD:(j + 1) * HD, hg, cols]).then_inc(ks_in[hg], 16)
                        if h == 0 and hg == 0:
                            for g in range(2):
                                load_q(sp, g)
                for g in range(2, GROUPS):
                    sp.wait_ge(scores, b * UNITS + (g - 1) * UPG)
                    load_q(sp, g)


        @block.gpsimd
        def _(pool):
            pool.memset(ident[:], 0.0).then_inc(pool_step, 1)
            pool.memset(pick[:], 0.0).then_inc(pool_step, 1)
            pool.memset(ones[:], 1.0).then_inc(consts, 1)
            pool.memset(mhalf[:], -0.5).then_inc(consts, 1)
            pool.memset(eps[:], EPS).then_inc(consts, 1)
            pool.wait_ge(pool_step, 2)
            pool.affine_select(out=ident[:], in_=ident[:], compare_op=ALU.not_equal, fill=1.0, base=0,
                               pattern=[[-1, P]], channel_multiplier=1).then_inc(consts, 1)
            for g in range(HPG):
                pool.affine_select(out=pick[:], in_=pick[:], compare_op=ALU.not_equal, fill=1.0,
                                   base=-g * HD, pattern=[[0, 1]], channel_multiplier=1).then_inc(pool_step, 1)
                pool.wait_ge(pool_step, 3 + g)
            pool.memset(rnorm[:], 0.0).then_inc(consts, 1)
            first = 2 + HPG
            per = 3

            with pool.Fori(0, B) as b:
                for h in range(2):
                    part_ = slice(h * TH, (h + 1) * TH)
                    pool.wait_ge(nsq_ready, b * 2 + h + 1)
                    pool.tensor_tensor(rnorm[:, part_], nsq[:, part_], mhalf[:, part_], ALU.pow) \
                        .then_inc(rnorm_ready, 1)
                    inverse_deviation(pool, b, h, part_, first + b * per + h)
                for h in range(2):
                    for t in range(h * TH, (h + 1) * TH):
                        if t == h * TH:
                            pool.wait_ge(bank_filled, b * len(JOBS) + filled(("x1T", h, C - 1)))
                        pool.tensor_tensor(x1[:, t], x1[:, t], bob[:], ALU.add).then_inc(x1b_ready, 1)
                inverse_deviation(pool, b, 2, slice(0, T), first + b * per + 2)


        @block.tensor
        def _(pe):
            mm = nc.tensor.matmul
            pe.sem_inc(pv_done, 1)

            def start_job(b, name):
                i = INDEX[name]
                if i >= RING:
                    e, n = drained(JOBS[i - RING][0])
                    pe.wait_ge(act_drained if e == "act" else dve_drained, 1 + b * DRAINS[e] + n)
                return PS[:, i % RING]

            def wait_drained(b, name):
                e, n = drained(name)
                pe.wait_ge(act_drained if e == "act" else dve_drained, 1 + b * DRAINS[e] + n)

            pe.wait_ge(consts, 5)
            pe.wait_ge(w_in, 16 * 14)
            for m in range(C):
                for c in range(C):
                    mm(PS[:, m, 0:D], w0[:, 0, c, m * P:(m + 1) * P], w0[:, 1, c, :],
                       start=(c == 0), stop=(c == C - 1)).then_inc(setup_pe, 1)
                    nc.tensor.transpose(PS[:, 2 + m, c * P:(c + 1) * P], w0[:, 2, c, m * P:(m + 1) * P],
                                        ident[:]).then_inc(setup_pe, 1)

            with pe.Fori(0, B) as b:
                pe.wait_ge(setup_dve, 2 * C)
                pe.wait_ge(mask_ready, 1)
                pe.wait_ge(act_drained, 1 + b * DRAINS["act"])
                pe.wait_ge(dve_drained, 1 + b * DRAINS["dve"])
                pe.wait_ge(x_in, b * 16 + 16)
                for c in range(C):
                    for q in range(2):
                        to = start_job(b, ("xT", c, q))
                        for i in range(TH):
                            last = nc.tensor.transpose(to[:, i * P:(i + 1) * P],
                                                       xs[:, q * TH + i, c * P:(c + 1) * P], ident[:])
                        last.then_inc(bank_filled, 1)
                wait_drained(b, ("xT", C - 1, 1))
                wait_drained(b, ("xT", C - 1, 0))
                for m in range(C):
                    for h in range(2):
                        to = start_job(b, ("G", m, h))
                        for c in range(C):
                            last = mm(to, A0[:, c, m * P:(m + 1) * P], xT[:, c, h * HALF:(h + 1) * HALF],
                                      start=(c == 0), stop=(c == C - 1))
                        last.then_inc(bank_filled, 1)
                for p in range(T // 2):
                    to = start_job(b, ("v0", p))
                    for i in range(2):
                        for c in range(C):
                            t = 2 * p + i
                            last = mm(to[:, i * D:(i + 1) * D], xT[:, c, t * P:(t + 1) * P], wv0T[:, c, :],
                                      start=(c == 0), stop=(c == C - 1))
                    last.then_inc(bank_filled, 1)

                def add_squares(h, m):
                    pe.wait_ge(squared, b * 2 * T + h * T + m + 1)
                    g = m % 4
                    mm(PS[g * HD:(g + 1) * HD, SUMS], ones[:], sq[:, m % 4],
                       start=(m < 4), stop=(m >= 4)).then_inc(sums_added, 1)

                def rel_tiles(h):
                    for m in range(T):
                        to = start_job(b, ("rel", h, m))
                        for c in range(C):
                            last = mm(to, xT[:, c, m * P:(m + 1) * P], GT[:, c, h * HALF:(h + 1) * HALF],
                                      start=(c == 0), stop=(c == C - 1))
                        last.then_inc(bank_filled, 1)
                        if m >= 2:
                            add_squares(h, m - 2)
                    add_squares(h, T - 2)
                    add_squares(h, T - 1)

                def norm_columns(h):
                    pe.wait_ge(sums_out, b * 2 + h + 1)
                    for t in range(TH):
                        last = mm(PS[:, COLS, t:t + 1], sums[:, t * P:(t + 1) * P], pick[:],
                                  start=True, stop=True)
                    last.then_inc(cols_ready, 1)

                def out_tiles(h):
                    wait_drained(b, ("rel", h, T - 1))
                    for t in range(TH):
                        to = start_job(b, ("out", h, t))
                        for m in range(T):
                            last = mm(to[:, 0:D], relm[h][:, m, t * P:(t + 1) * P], v0[:, m, :],
                                      start=(m == 0), stop=(m == T - 1))
                        last.then_inc(bank_filled, 1)
                        if t == 0:
                            norm_columns(h)

                def project(h):
                    pe.wait_ge(x1_ready, 1 + b * T + (h + 1) * TH)
                    for c in range(C):
                        to = start_job(b, ("x1T", h, c))
                        for i in range(TH):
                            last = nc.tensor.transpose(to[:, i * P:(i + 1) * P],
                                                       x1[:, h * TH + i, c * P:(c + 1) * P], ident[:])
                        last.then_inc(bank_filled, 1)
                    wait_drained(b, ("x1T", h, C - 1))
                    for w in range(2 * HG):
                        hg, q = divmod(w, 2)
                        to = start_job(b, ("qk", h, w))
                        for c in range(C):
                            last = mm(to, (wq if q else wk)[:, c, hg * P:(hg + 1) * P],
                                      x1T[:, c, h * HALF:(h + 1) * HALF], start=(c == 0), stop=(c == C - 1))
                        last.then_inc(bank_filled, 1)

                def values(h):
                    for p in range(TH // 2):
                        to = start_job(b, ("v1", h, p))
                        for i in range(2):
                            t = h * TH + 2 * p + i
                            for c in range(C):
                                last = mm(to[:, i * D:(i + 1) * D], x1T[:, c, t * P:(t + 1) * P], wv[:, c, :],
                                          start=(c == 0), stop=(c == C - 1))
                        last.then_inc(bank_filled, 1)

                wait_drained(b, ("G", C - 1, 1))
                wait_drained(b, ("G", C - 1, 0))
                rel_tiles(0)
                wait_drained(b, ("v0", T // 2 - 1))
                wait_drained(b, ("v0", T // 2 - 2))
                out_tiles(0)
                rel_tiles(1)
                project(0)
                out_tiles(1)
                values(0)
                project(1)
                values(1)

                def score(u):
                    g, hg, q0, qi, j = unit(u)
                    if u >= 2:
                        pe.wait_ge(masked, b * UNITS + u - 1)
                    if u % UPG == 0:
                        pe.wait_ge(qs_in[g % 2], (b * (GROUPS // 2) + g // 2 + 1) * 16 * 4 * HPG)
                    if u % (UNITS // HG) == 0:
                        pe.wait_ge(ks_in[hg], (b + 1) * 16 * 2 * 4 * HPG)
                    for h in range(2):
                        last = mm(PS[:, 2 * (u % 2) + h], QS[:, g % 2, j, qi * P:(qi + 1) * P].bitcast(F32R),
                                  KS[:, hg * HPG + j, h * HALF:(h + 1) * HALF].bitcast(F32R),
                                  start=True, stop=True)
                    last.then_inc(scores, 1)

                def turn(u):
                    pe.wait_ge(probs, b * UNITS + u + 1)
                    for k, (free, done) in enumerate(((pt_a, turned_a), (pt_b, turned_b))):
                        pe.wait_ge(free, 1 + b * UNITS + u)
                        for i in range(TH):
                            t = k * TH + i
                            last = nc.tensor.transpose(PS[:, 4 + k, i * P:(i + 1) * P],
                                                       nr[:, u % NRING, t * P:(t + 1) * P], ident[:])
                        last.then_inc(done, 1)

                def outputs(g, t):
                    hg = unit(g * UPG)[1]
                    if t == 0:
                        pe.wait_ge(pt_a, 1 + b * UNITS + (g + 1) * UPG)
                        pe.wait_ge(pt_b, 1 + b * UNITS + (g + 1) * UPG)
                        pe.wait_ge(o_ready, 1 + b * GROUPS + g)
                    for j in range(HPG):
                        h = hg * HPG + j
                        last = mm(PS[j * HD:(j + 1) * HD, SUMS, 0:GQ], vs[:, t, h * HD:(h + 1) * HD],
                                  pt[:, g % 2, j, t, :], start=(t == 0), stop=(t == T - 1))
                    if t == T - 1:
                        last.then_inc(pv_done, 1)

                def turn_rowsums(g):
                    pe.wait_ge(rexp_ready, b * GROUPS + g + 1)
                    pe.wait_ge(rT_ready, 1 + b * GROUPS + g)
                    for qi in range(QT):
                        last = nc.tensor.transpose(PS[:, COLS, qi * P:(qi + 1) * P],
                                                   rexp[:, qi].rearrange("p j d -> p (j d)"), ident[:])
                    last.then_inc(rT_filled, 1)

                wait_drained(b, ("qk", 1, 2 * HG - 1))
                wait_drained(b, ("v1", 1, TH // 2 - 1))
                score(0)
                score(1)
                for u in range(UNITS):
                    g, r = divmod(u, UPG)
                    if u + 2 < UNITS:
                        score(u + 2)
                    turn(u)
                    if g >= 1:
                        if r == 4:
                            turn_rowsums(g - 1)
                        outputs(g - 1, r)
                turn_rowsums(GROUPS - 1)
                for t in range(T):
                    outputs(GROUPS - 1, t)

                pe.wait_ge(o_ready, 1 + b * GROUPS + GROUPS)
                for p in range(T // 2):
                    to = start_job(b, ("wo", p))
                    for i in range(2):
                        t = 2 * p + i
                        for c in range(C):
                            last = mm(to[:, i * D:(i + 1) * D], QO[:, c, t * P:(t + 1) * P], wo[:, c, :],
                                      start=(c == 0), stop=(c == C - 1))
                    last.then_inc(bank_filled, 1)

        @block.scalar
        def _(act):
            for s in (act_drained, pt_a, rT_ready):
                act.sem_inc(s, 1)
            act.sem_inc(out_done, 16)
            with act.Fori(0, B) as b:
                def fill_wait(name):
                    act.wait_ge(bank_filled, b * len(JOBS) + filled(name))
                    return PS[:, bank(name)]

                for c in range(C):
                    for q in range(2):
                        if (c + q) % 2:
                            act.activation(xT[:, c, q * HALF:(q + 1) * HALF], fill_wait(("xT", c, q)),
                                           ACT.Copy).then_inc(act_drained, 1)
                for m in range(C):
                    for h in range(2):
                        if (m + h) % 2:
                            act.activation(GT[:, m, h * HALF:(h + 1) * HALF], fill_wait(("G", m, h)),
                                           ACT.Copy).then_inc(act_drained, 1)
                for p in range(1, T // 2, 2):
                    act.activation(v0[:, 2 * p:2 * p + 2, :].rearrange("p t d -> p (t d)"),
                                   fill_wait(("v0", p)), ACT.Copy).then_inc(act_drained, 1)

                def squares(h):
                    for m in range(T):
                        i = h * T + m
                        act.wait_ge(dve_drained, 1 + b * DRAINS["dve"] + drained(("rel", h, m))[1])
                        if i >= 4:
                            act.wait_ge(sums_added, b * 2 * T + i - 3)
                        act.activation(sq[:, i % 4], relm[h][:, m], ACT.Square).then_inc(squared, 1)
                    act.wait_ge(sums_added, b * 2 * T + (h + 1) * T)
                    if h:
                        act.wait_ge(cols_ready, b * 2 + h)
                    act.activation(sums, PS[:, SUMS], ACT.Copy).then_inc(sums_out, 1)

                def drain_project(h):
                    for c in range(C):
                        act.activation(x1T[:, c, h * HALF:(h + 1) * HALF], fill_wait(("x1T", h, c)),
                                       ACT.Copy).then_inc(act_drained, 1)
                    for w in range(2 * HG):
                        hg, q = divmod(w, 2)
                        n = h * 2 * HG + w
                        if n >= 2:
                            act.wait_ge(lo_ready, b * 4 * HG + n - 1)
                        src = fill_wait(("qk", h, w))
                        if q:
                            ins = act.activation(qf[:, n % 2], src, ACT.Identity, bias=bqc[:, hg:hg + 1], scale=QSCALE)
                        else:
                            ins = act.activation(qf[:, n % 2], src, ACT.Identity, bias=bkc[:, hg:hg + 1], scale=1.0)
                        ins.then_inc(act_drained, 1)
                        act.wait_ge(act_drained, 1 + b * DRAINS["act"] + drained(("qk", h, w))[1])
                        act.activation((qhi if q else khi)[:, hg, h * HALF:(h + 1) * HALF].bitcast(F32R), qf[:, n % 2],
                                       ACT.Copy).then_inc(hi_ready, 1)

                squares(0)
                squares(1)
                drain_project(0)
                drain_project(1)

                def exps(u):
                    act.wait_ge(masked, b * UNITS + u + 1)
                    act.activation(nr[:, u % NRING], nr[:, u % NRING], ACT.Exp, bias=least[:, u:u + 1],
                                   scale=-1.0, accum_out=rowsum[:, u:u + 1]).then_inc(probs, 1)

                exps(0)
                exps(1)
                for u in range(UNITS):
                    g, r = divmod(u, UPG)
                    _, _, _, qi, j = unit(u)
                    if u == UPG:
                        for s in ks_in:
                            act.wait_ge(s, (b + 1) * 16 * 2 * 4 * HPG)
                    if r == 0 and g >= 2:
                        act.wait_ge(pv_done, 1 + b * GROUPS + g - 1)
                    act.wait_ge(turned_a, b * UNITS + u + 1)
                    act.activation(pt[:, g % 2, j, 0:TH, qi * P:(qi + 1) * P],
                                   PS[:, 4].rearrange("p (t q) -> p t q", q=P), ACT.Copy).then_inc(pt_a, 1)
                    if u + 2 < UNITS:
                        exps(u + 2)
                    if g >= 1 and r == 6:
                        rowsums_out(act, b, g - 1)
                rowsums_out(act, b, GROUPS - 1)
                act.wait_ge(y_ready, (b + 1) * T)
                act.dma_start(ov[bass.ds(b, 1)].rearrange("o p t d -> p (o t) d"), x1[:]).then_inc(out_done, 16)
            act.wait_ge(out_done, 16 + B * 16)


        @block.vector
        def _(dve):
            v = nc.vector
            for s in (dve_drained, pt_b, o_ready, x1_ready):
                dve.sem_inc(s, 1)
            dve.wait_ge(w_in, 16 * 14)
            v.tensor_scalar(negmask[:], negmask[:], 1.0, -MASK, ALU.subtract, ALU.mult).then_inc(mask_ready, 1)
            v.tensor_scalar(bqc[:], bqc[:], QSCALE, None, ALU.mult).then_inc(setup_dve, 1)
            dve.wait_ge(setup_pe, 2 * C * C)
            for m in range(C):
                last = v.tensor_copy(A0[:, m, :], PS[:, m, 0:D])
                v.tensor_copy(wv0T[:, m, :], PS[:, 2 + m, 0:D]).then_inc(setup_dve, 1)
            last.then_inc(setup_dve, 1)
            STEPS = 3 * T + 1

            with dve.Fori(0, B) as b:
                def fill_wait(name):
                    dve.wait_ge(bank_filled, b * len(JOBS) + filled(name))
                    return PS[:, bank(name)]

                for c in range(C):
                    for q in range(2):
                        if not (c + q) % 2:
                            v.tensor_copy(xT[:, c, q * HALF:(q + 1) * HALF], fill_wait(("xT", c, q))) \
                                .then_inc(dve_drained, 1)
                for m in range(C):
                    for h in range(2):
                        if not (m + h) % 2:
                            v.tensor_copy(GT[:, m, h * HALF:(h + 1) * HALF], fill_wait(("G", m, h))) \
                                .then_inc(dve_drained, 1)
                for p in range(0, T // 2, 2):
                    v.tensor_copy(v0[:, 2 * p:2 * p + 2, :].rearrange("p t d -> p (t d)"),
                                  fill_wait(("v0", p))).then_inc(dve_drained, 1)

                def mask_rel(h):
                    for m in range(T):
                        i = h * T + m
                        dve.wait_ge(adj_in[i % ADJ], (b * (2 * T // ADJ) + i // ADJ + 1) * 16)
                        v.tensor_tensor(relm[h][:, m], fill_wait(("rel", h, m)), adjr[:, i % ADJ], ALU.mult) \
                            .then_inc(dve_drained, 1)

                def norm_out(h):
                    dve.wait_ge(cols_ready, b * 2 + h + 1)
                    v.tensor_copy(nsq[:, h * TH:(h + 1) * TH], PS[:, COLS, 0:TH]).then_inc(nsq_ready, 1)

                def residual(h):
                    dve.wait_ge(rnorm_ready, b * 2 + h + 1)
                    if h == 0:
                        dve.wait_ge(out_done, 16 + b * 16)
                    for i in range(TH):
                        t = h * TH + i
                        v.scalar_tensor_tensor(out=x1[:, t], in0=fill_wait(("out", h, i))[:, 0:D],
                                               scalar=rnorm[:, t:t + 1], in1=xs[:, t], op0=ALU.mult,
                                               op1=ALU.add).then_inc(dve_drained, 1)
                        dve.wait_ge(dve_drained, 1 + b * DRAINS["dve"] + drained(("out", h, i))[1])
                        v.bn_stats(stats[:, t], x1[:, t]).then_inc(stat_step, 1)
                    alone(dve, stat_step, b * 2 * T + (h + 1) * TH)
                    for i in range(TH):
                        t = h * TH + i
                        last = v.bn_aggr(mv[:, t], stats[:, t])
                    last.then_inc(var_ready, 1)
                    dve.wait_ge(rstd_ready, b * 3 + h + 1)
                    for i in range(TH):
                        t = h * TH + i
                        v.tensor_scalar(x1[:, t], x1[:, t], mv[:, t, 0:1], rstd[:, t:t + 1],
                                        ALU.subtract, ALU.mult).then_inc(x1_ready, 1)

                def cut(h):
                    for w in range(2 * HG):
                        hg, q = divmod(w, 2)
                        n = h * 2 * HG + w
                        cols = slice(h * HALF, (h + 1) * HALF)
                        dve.wait_ge(hi_ready, b * 4 * HG + n + 1)
                        hi = (qhi if q else khi)[:, hg, cols]
                        v.tensor_tensor((qlo if q else klo)[:, hg, cols].bitcast(F32R), qf[:, n % 2], hi, ALU.subtract) \
                            .then_inc(lo_ready, 1)

                def add_bv(h):
                    for p in range(TH // 2):
                        t = h * TH + 2 * p
                        src = fill_wait(("v1", h, p)).rearrange("p (t d) -> p t d", d=D)
                        v.tensor_tensor(vs[:, t:t + 2, :], src, bvb[:].rearrange("p (a d) -> p a d", a=1)
                                        .to_broadcast([P, 2, D]), ALU.add).then_inc(dve_drained, 1)

                mask_rel(0)
                norm_out(0)
                residual(0)
                mask_rel(1)
                cut(0)
                norm_out(1)
                residual(1)
                add_bv(0)
                cut(1)
                add_bv(1)

                def mask_scores(u):
                    _, _, q0, qi, _ = unit(u)
                    if u >= NRING:
                        dve.wait_ge(turned_b, b * UNITS + u - NRING + 1)
                    alone(dve, scores, b * UNITS + u + 1)
                    k = 2 * (u % 2)
                    v.tensor_tensor_reduce(out=nr[:, u % NRING], in0=PS[:, k:k + 2].rearrange("p k n -> p (k n)"),
                                           in1=negmask[:, q0 // P + qi], scale=1.0, scalar=3.0e38,
                                           op0=ALU.add, op1=ALU.min,
                                           accum_out=least[:, u:u + 1]).then_inc(masked, 1)

                def rowsums(g):
                    dve.wait_ge(probs, b * UNITS + (g + 1) * UPG)
                    if g:
                        dve.wait_ge(rT_filled, b * GROUPS + g)
                    v.reciprocal(rrow[:], rowsum[:, g * UPG:(g + 1) * UPG]).then_inc(rrow_ready, 1)
                    dve.wait_ge(rrow_ready, b * GROUPS + g + 1)
                    v.tensor_copy(rexp[:], rrow[:].rearrange("p (q j a) -> p q j a", q=QT, a=1)
                                  .to_broadcast([P, QT, HPG, HD])).then_inc(rexp_ready, 1)

                def group_out(g):
                    _, hg, q0, _, _ = unit(g * UPG)
                    dve.wait_ge(pv_done, 1 + b * GROUPS + g + 1)
                    dve.wait_ge(rT_ready, 1 + b * GROUPS + g + 1)
                    v.tensor_tensor(QO[:, hg, q0:q0 + GQ], PS[:, SUMS, 0:GQ], rT[:], ALU.mult) \
                        .then_inc(o_ready, 1)

                mask_scores(0)
                mask_scores(1)
                for u in range(UNITS):
                    g, r = divmod(u, UPG)
                    _, _, _, qi, j = unit(u)
                    if u + 2 < UNITS:
                        mask_scores(u + 2)
                    if u == UPG:
                        for s in ks_in:
                            dve.wait_ge(s, (b + 1) * 16 * 2 * 4 * HPG)
                    if r == 0 and g >= 2:
                        group_out(g - 2)
                    dve.wait_ge(turned_b, b * UNITS + u + 1)
                    v.tensor_copy(pt[:, g % 2, j, TH:T, qi * P:(qi + 1) * P],
                                  PS[:, 5].rearrange("p (t q) -> p t q", q=P)).then_inc(pt_b, 1)
                    if r == 1 and g >= 1:
                        rowsums(g - 1)
                rowsums(GROUPS - 1)
                group_out(GROUPS - 2)
                group_out(GROUPS - 1)

                dve.wait_ge(x1b_ready, (b + 1) * T)
                for p in range(T // 2):
                    src = fill_wait(("wo", p))
                    dst = x1[:, 2 * p:2 * p + 2, :].rearrange("p t d -> p (t d)")
                    v.tensor_tensor(dst, src, dst, ALU.add).then_inc(dve_drained, 1)
                    dve.wait_ge(dve_drained, 1 + b * DRAINS["dve"] + drained(("wo", p))[1])
                    for t in (2 * p, 2 * p + 1):
                        v.bn_stats(stats[:, t], x1[:, t]).then_inc(stat_step, 1)
                alone(dve, stat_step, (b + 1) * 2 * T)
                for t in range(T):
                    last = v.bn_aggr(mv[:, t], stats[:, t])
                last.then_inc(var_ready, 1)
                dve.wait_ge(rstd_ready, b * 3 + 3)
                for t in range(T):
                    v.tensor_scalar(x1[:, t], x1[:, t], mv[:, t, 0:1], rstd[:, t:t + 1],
                                    ALU.subtract, ALU.mult).then_inc(y_ready, 1)


_INS = ["x", "adj", "L0_gnn_Wq", "L0_gnn_Wk", "L0_gnn_Wv", "L1_gnn_Wq", "L1_gnn_bq", "L1_gnn_Wk", "L1_gnn_bk",
        "L1_gnn_Wv", "L1_gnn_bv", "L1_gnn_Wo", "L1_gnn_bo"]


def kernel(**inputs):
    import concourse.bacc as bacc
    from concourse.bass_utils import run_bass_kernel_spmd

    nc = bacc.Bacc("TRN2", target_bir_lowering=False, num_devices=1)
    arrays, args = {}, []
    for name in _INS:
        a = np.ascontiguousarray(inputs[name])
        arrays[f"in_{name}"] = a
        args.append(nc.dram_tensor(f"in_{name}", a.shape, mybir.dt.from_np(a.dtype), kind="ExternalInput").ap())
    out = nc.dram_tensor("out_0", (B, N, D), F32, kind="ExternalOutput").ap()
    build(nc, *args, out)
    r = run_bass_kernel_spmd(nc, [arrays], core_ids=[0])
    return r.results[0]["out_0"]
```

```python
from contextlib import ExitStack

import numpy as np

import concourse.bass as bass
from concourse import mybir

ALU = mybir.AluOpType
ACT = mybir.ActivationFunctionType
F32 = mybir.dt.float32
F32R = mybir.dt.float32r

B, N, D, H = 8, 1024, 256, 8
HD = D // H
P = 128
C = D // P
T = N // P
HALF = 512
TH = HALF // P
HPG = P // HD
HG = H // HPG
GQ = 256
QT = GQ // P
UPG = QT * HPG
GROUPS = HG * (N // GQ)
UNITS = GROUPS * UPG
MASK = 1.0e9
EPS = 1e-5
QSCALE = -1.0 / float(np.sqrt(np.float32(HD)))
RING = 6
SUMS, COLS = 6, 7
WO_BANK = (COLS, COLS, 0, 2)
NRING = 3
ADJ = 4


def job_list():
    jobs = [(("xT", c, q), "dve") for q in range(2) for c in range(C)]
    jobs += [(("G", 0, m), "dve") for m in range(C)]
    jobs += [(("v0", p), "dve") for p in range(T // 2)]
    jobs += [(("rel", 0, m), "dve") for m in range(T)]
    jobs += [(("G", 1, m), "dve") for m in range(C)]
    jobs += [(("out", 0, t), "dve") for t in range(TH)]
    jobs += [(("rel", 1, m), "dve") for m in range(T)]
    jobs += [(("x1T", 0, c), "act") for c in range(C)]
    jobs += [(("qk", 0, w), "act") for w in range(2 * HG)]
    jobs += [(("out", 1, t), "dve") for t in range(TH)]
    jobs += [(("v1", 0, p), "dve") for p in range(TH // 2)]
    jobs += [(("x1T", 1, c), "act") for c in range(C)]
    jobs += [(("qk", 1, w), "act") for w in range(2 * HG)]
    jobs += [(("v1", 1, p), "dve") for p in range(TH // 2)]
    return jobs


JOBS = job_list()
CUT = [name for name, _ in JOBS if name[0] in ("xT", "G", "v0", "rel")]
INDEX = {name: i for i, (name, _) in enumerate(JOBS)}
DRAINS = {e: sum(1 for _, x in JOBS if x == e) for e in ("act", "dve")}


def bank(name):
    return INDEX[name] % RING


def filled(name):
    return INDEX[name] + 1


def drained(name):
    i = INDEX[name]
    e = JOBS[i][1]
    return e, sum(1 for _, x in JOBS[:i + 1] if x == e)


def cut_high(name):
    return CUT.index(name) + 1


def unit(u):
    g, r = divmod(u, UPG)
    hg, qp = divmod(g, N // GQ)
    qi, j = divmod(r, HPG)
    return g, hg, qp * GQ, qi, j


def build(nc, x, adj, wq0, wk0, wv0, wq1, bq1, wk1, bk1, wv1, bv1, wo1, bo1, out):
    with ExitStack() as ctx:
        def sb(name, shape, dt=F32):
            return ctx.enter_context(nc.sbuf_tensor(name, shape, dt))

        def sem(name):
            return ctx.enter_context(nc.semaphore(name))

        PS = ctx.enter_context(nc.psum_tensor("PS", [P, 8, HALF], F32))

        def overlay(size, *sets):
            found = []
            for one in sets:
                with ExitStack() as place:
                    for name, shape, dt in one:
                        found.append(place.enter_context(nc.sbuf_tensor(name, shape, dt)))
            sb(sets[0][0][0] + "_place", [P, size])
            return found

        negmask = sb("negmask", [P, T, N])
        A0 = sb("A0", [P, 2, C, D], F32R)
        wv0T = sb("wv0T", [P, 2, C, D], F32R)
        wq = sb("wq", [P, C, D])
        wk = sb("wk", [P, C, D])
        wv = sb("wv", [P, C, D])
        wo = sb("wo", [P, C, D])
        bqc = sb("bqc", [P, C])
        bkc = sb("bkc", [P, C])
        bvb = sb("bvb", [P, D])
        bob = sb("bob", [P, D])
        ident = sb("ident", [P, P])
        ones = sb("ones", [P, HD])
        pick = sb("pick", [P, 1])
        mhalf = sb("mhalf", [P, T])
        minus = sb("minus", [P, T])
        eps = sb("eps", [P, T])
        xs = sb("xs", [P, T, D])
        x1 = sb("x1", [P, T, D])
        qhi = QO = sb("QO", [P, HG, N])
        qlo = sb("qlo", [P, HG, N])
        k0 = sb("k0", [P, 2, N])
        QS = sb("QS", [P, 2, HPG, GQ])
        KS0 = sb("KS0", [P, HPG, N])
        vs, v0h = overlay(T * D, [("vs", [P, T, D], F32)], [("v0h", [P, T, D], F32R)])
        KS1, adjr, sq, rf = overlay(
            HPG * N,
            [("KS1", [P, HPG, N], F32)],
            [("adjr", [P, ADJ, HALF], F32),
             ("sq", [P, 2, HALF], F32),
             ("rf", [P, 2, HALF], F32)])
        pt, nr, rel, k1, xT, v0l, G, sums, _, x1T = overlay(
            2 * HPG * T * GQ + NRING * N,
            [("pt", [P, 2, HPG, T, GQ], F32), ("nr", [P, NRING, N], F32)],
            [("rel", [P, 2, T, HALF], F32R),
             ("k1", [P, 2, N], F32),
             ("xT", [P, 2, C, N], F32R),
             ("v0l", [P, T, D], F32R),
             ("G", [P, 2, C, HALF], F32R),
             ("sums", [P, HALF], F32)],
            [("before_x1T", [P, 2 * HPG * T * GQ], F32), ("x1T", [P, C, N], F32)])
        stats = sb("stats", [P, T, 6])
        nsq = sb("nsq", [P, T])
        rnorm = sb("rnorm", [P, T])
        mv = sb("mv", [P, T, 2])
        rstd = sb("rstd", [P, T])
        shift = sb("shift", [P, T])
        least = sb("least", [P, UNITS])
        rowsum = sb("rowsum", [P, UNITS])
        rrow = sb("rrow", [P, UPG])
        rexp = sb("rexp", [P, QT, HPG, HD])
        rT = sb("rT", [P, GQ])
        v0 = (v0h, v0l)
        w0 = pt[:, 0, 0, 0:6].rearrange("p (w c) d -> p w c d", c=C)

        passed = sem("passed")
        w_in = sem("w_in")
        consts = sem("consts")
        setup_pe = sem("setup_pe")
        setup_high = sem("setup_high")
        setup_dve = sem("setup_dve")
        mask_ready = sem("mask_ready")
        x_in = sem("x_in")
        adj_in = [sem(f"adj_in{k}") for k in range(ADJ)]
        bank_filled = sem("bank_filled")
        high = sem("high")
        act_drained = sem("act_drained")
        dve_drained = sem("dve_drained")
        rel_cut = sem("rel_cut")
        squared = sem("squared")
        sums_added = sem("sums_added")
        sums_out = sem("sums_out")
        cols_ready = sem("cols_ready")
        nsq_ready = sem("nsq_ready")
        rnorm_ready = sem("rnorm_ready")
        stat_step = sem("stat_step")
        var_ready = sem("var_ready")
        pool_step = sem("pool_step")
        rstd_ready = sem("rstd_ready")
        x1_ready = sem("x1_ready")
        x1b_ready = sem("x1b_ready")
        hi_ready = sem("hi_ready")
        lo_ready = sem("lo_ready")
        ks_in = [sem(f"ks_in{g}") for g in range(HG)]
        qs_in = [sem(f"qs_in{g}") for g in range(2)]
        scores = sem("scores")
        masked = sem("masked")
        probs = sem("probs")
        turned_a = sem("turned_a")
        turned_b = sem("turned_b")
        pt_a = sem("pt_a")
        pt_b = sem("pt_b")
        rrow_ready = sem("rrow_ready")
        rexp_ready = sem("rexp_ready")
        rT_filled = sem("rT_filled")
        rT_ready = sem("rT_ready")
        pv_done = sem("pv_done")
        o_ready = sem("o_ready")
        wo_filled = sem("wo_filled")
        wo_drained = sem("wo_drained")
        y_ready = sem("y_ready")
        out_done = sem("out_done")

        block = ctx.enter_context(nc.Block())
        xv = x.rearrange("b (t p) d -> b p t d", p=P)
        ov = out.rearrange("b (t p) d -> b p t d", p=P)
        adjv = adj.rearrange("(t p) n -> p t n", p=P)
        wview = lambda w: w.rearrange("(c p) e -> p c e", p=P)
        row = lambda v: v.rearrange("(a n) -> a n", a=1)
        K_LOADS = 16 * 2 * 4 * HPG

        def alone(eng, signal, value):
            eng.wait_ge(signal, value)
            eng.sem_inc(passed, 1)

        def load_x(sp, b):
            sp.dma_start(xs[:], xv[bass.ds(b, 1)].rearrange("o p t d -> p (o t) d")).then_inc(x_in, 16)

        def load_k(sp, hg, cols, inc):
            for j in range(HPG):
                for r in range(4):
                    sp.dma_start((KS1 if hg else KS0)[r * HD:(r + 1) * HD, j, cols],
                                 (k1 if hg else k0)[j * HD:(j + 1) * HD, r % 2, cols]).then_inc(ks_in[hg], inc)

        def load_q(sp, g):
            _, hg, q0, _, _ = unit(g * UPG)
            for j in range(HPG):
                for r, src in enumerate((qhi, qhi, qlo, qlo)):
                    sp.dma_start(QS[r * HD:(r + 1) * HD, g % 2, j, :],
                                 src[j * HD:(j + 1) * HD, hg, q0:q0 + GQ]).then_inc(qs_in[g % 2], 16)

        @block.sync
        def _(sp):
            for w, src in enumerate((wq0, wk0, wv0)):
                sp.dma_start(w0[:, w], wview(src)).then_inc(w_in, 16)
            load_x(sp, 0)
            for dst, src in ((wq, wq1), (wk, wk1), (wv, wv1), (wo, wo1)):
                sp.dma_start(dst[:], wview(src)).then_inc(w_in, 16)
            for dst, src in ((bvb, bv1), (bob, bo1)):
                sp.dma_start(dst[:], row(src).to_broadcast([P, D])).then_inc(w_in, 16)
            for dst, src in ((bqc, bq1), (bkc, bk1)):
                for c in range(C):
                    sp.dma_start(dst[:, c:c + 1], src[c * P:(c + 1) * P].rearrange("(p a) -> p a", a=1)) \
                      .then_inc(w_in, 16)
            sp.dma_start(negmask[:], adjv).then_inc(w_in, 16)
            with sp.Fori(0, B) as b:
                for h in range(2):
                    for m in range(T):
                        i = h * T + m
                        if i == 0:
                            sp.wait_ge(scores, 1 + b * UNITS)
                        if i >= ADJ:
                            h0, m0 = divmod(i - ADJ, T)
                            sp.wait_ge(dve_drained, 1 + b * DRAINS["dve"] + drained(("rel", h0, m0))[1])
                        sp.dma_start(adjr[:, i % ADJ], adjv[:, m, h * HALF:(h + 1) * HALF]) \
                          .then_inc(adj_in[i % ADJ], 16)
                first, second = slice(0, HALF), slice(HALF, N)
                sp.wait_ge(lo_ready, b * 4 * HG + 1)
                load_k(sp, 0, first, 16)
                sp.wait_ge(lo_ready, b * 4 * HG + 2)
                load_q(sp, 0)
                load_q(sp, 1)
                sp.wait_ge(lo_ready, b * 4 * HG + 2 * HG + 1)
                load_k(sp, 0, second, 16)
                sp.wait_ge(lo_ready, (b + 1) * 4 * HG)
                load_k(sp, 1, slice(0, N), 32)
                sp.wait_ge(x1_ready, 1 + (b + 1) * T)
                load_x(sp, (b + 1) % B)
                for g in range(2, GROUPS):
                    sp.wait_ge(scores, 1 + b * UNITS + (g - 1) * UPG)
                    load_q(sp, g)
                sp.wait_ge(y_ready, (b + 1) * T)
                sp.dma_start(ov[bass.ds(b, 1)].rearrange("o p t d -> p (o t) d"), x1[:]).then_inc(out_done, 16)
            sp.wait_ge(x_in, (B + 1) * 16)
            sp.wait_ge(out_done, 16 + B * 16)

        def inverse_deviation(pool, b, k, tiles, steps):
            pool.wait_ge(var_ready, b * 3 + k + 1)
            pool.tensor_tensor(rstd[:, tiles], mv[:, tiles, 1], eps[:, tiles], ALU.add).then_inc(pool_step, 1)
            pool.wait_ge(pool_step, steps + 1)
            return pool.tensor_tensor(rstd[:, tiles], rstd[:, tiles], mhalf[:, tiles], ALU.pow)

        @block.gpsimd
        def _(pool):
            pool.memset(ident[:], 0.0).then_inc(pool_step, 1)
            pool.memset(pick[:], 0.0).then_inc(pool_step, 1)
            for dst, value in ((ones, 1.0), (mhalf, -0.5), (eps, EPS), (minus, -1.0)):
                pool.memset(dst[:], value).then_inc(consts, 1)
            pool.wait_ge(pool_step, 2)
            pool.affine_select(out=ident[:], in_=ident[:], compare_op=ALU.not_equal, fill=1.0, base=0,
                               pattern=[[-1, P]], channel_multiplier=1).then_inc(consts, 1)
            for g in range(HPG):
                pool.affine_select(out=pick[:], in_=pick[:], compare_op=ALU.not_equal, fill=1.0,
                                   base=-g * HD, pattern=[[0, 1]], channel_multiplier=1).then_inc(pool_step, 1)
                pool.wait_ge(pool_step, 3 + g)
            pool.memset(rnorm[:], 0.0).then_inc(consts, 1)
            first = 2 + HPG
            per = 6

            with pool.Fori(0, B) as b:
                for h in range(2):
                    tiles = slice(h * TH, (h + 1) * TH)
                    pool.wait_ge(nsq_ready, b * 2 + h + 1)
                    pool.tensor_tensor(rnorm[:, tiles], nsq[:, tiles], mhalf[:, tiles], ALU.pow) \
                        .then_inc(rnorm_ready, 1)
                    inverse_deviation(pool, b, h, tiles, first + b * per + h).then_inc(rstd_ready, 1)
                for h in range(2):
                    for t in range(h * TH, (h + 1) * TH):
                        if t == h * TH:
                            pool.wait_ge(bank_filled, b * len(JOBS) + filled(("x1T", h, C - 1)))
                        pool.tensor_tensor(x1[:, t], x1[:, t], bob[:], ALU.add).then_inc(x1b_ready, 1)
                for g in range(GROUPS):
                    pool.wait_ge(probs, b * UNITS + (g + 1) * UPG)
                    pool.tensor_tensor(rrow[:], rowsum[:, g * UPG:(g + 1) * UPG], minus[:], ALU.pow) \
                        .then_inc(rrow_ready, 1)
                    alone(pool, rT_filled, 1 + b * GROUPS + g)
                    alone(pool, rrow_ready, b * GROUPS + g + 1)
                    pool.tensor_copy(rexp[:], rrow[:].rearrange("p (q j a) -> p q j a", q=QT, a=1)
                                     .to_broadcast([P, QT, HPG, HD])).then_inc(rexp_ready, 1)
                steps = first + b * per + 2
                inverse_deviation(pool, b, 2, slice(0, T), steps).then_inc(pool_step, 1)
                pool.wait_ge(pool_step, steps + 2)
                pool.tensor_tensor(shift[:], mv[:, :, 0], rstd[:], ALU.mult).then_inc(pool_step, 1)
                pool.wait_ge(pool_step, steps + 3)
                pool.tensor_tensor(shift[:], shift[:], minus[:], ALU.mult).then_inc(pool_step, 1)
                alone(pool, pool_step, steps + 4)
                for t in range(T):
                    pool.tensor_scalar(x1[:, t], x1[:, t], rstd[:, t:t + 1], shift[:, t:t + 1],
                                       ALU.mult, ALU.add).then_inc(y_ready, 1)

        @block.tensor
        def _(pe):
            mm = nc.tensor.matmul
            for s in (pv_done, scores, rT_filled):
                pe.sem_inc(s, 1)

            def wait_drained(b, name):
                e, n = drained(name)
                pe.wait_ge(act_drained if e == "act" else dve_drained, 1 + b * DRAINS[e] + n)

            def start_job(b, name):
                i = INDEX[name]
                if i >= RING:
                    wait_drained(b, JOBS[i - RING][0])
                return PS[:, i % RING]

            def three_passes(to, stationary, moving, first, final):
                for n, (r, k) in enumerate(((0, 0), (0, 1), (1, 0))):
                    last = mm(to, stationary(r), moving(k), start=first and n == 0, stop=final and n == 2)
                return last

            pe.wait_ge(consts, 6)
            pe.wait_ge(w_in, 16 * 14)
            for m in range(C):
                for c in range(C):
                    mm(PS[:, m, 0:D], w0[:, 0, c, m * P:(m + 1) * P], w0[:, 1, c, :],
                       start=(c == 0), stop=(c == C - 1)).then_inc(setup_pe, 1)
                    nc.tensor.transpose(PS[:, 2 + m, c * P:(c + 1) * P], w0[:, 2, c, m * P:(m + 1) * P],
                                        ident[:]).then_inc(setup_pe, 1)
            pe.wait_ge(setup_dve, 2 * C + 1)
            pe.wait_ge(mask_ready, 1)

            with pe.Fori(0, B) as b:
                pe.wait_ge(pt_a, 1 + b * UNITS)
                pe.wait_ge(wo_drained, 1 + b * (T // 2))
                pe.wait_ge(x_in, b * 16 + 16)
                for q in range(2):
                    for c in range(C):
                        to = start_job(b, ("xT", c, q))
                        for i in range(TH):
                            last = nc.tensor.transpose(to[:, i * P:(i + 1) * P],
                                                       xs[:, q * TH + i, c * P:(c + 1) * P], ident[:])
                        last.then_inc(bank_filled, 1)

                def project_g(h):
                    cols = slice(h * HALF, (h + 1) * HALF)
                    for m in range(C):
                        to = start_job(b, ("G", h, m))
                        for c in range(C):
                            last = three_passes(to, lambda r: A0[:, r, c, m * P:(m + 1) * P],
                                                lambda k: xT[:, k, c, cols], c == 0, c == C - 1)
                        last.then_inc(bank_filled, 1)

                wait_drained(b, ("xT", C - 1, 0))
                project_g(0)
                wait_drained(b, ("xT", C - 1, 1))
                for p in range(T // 2):
                    to = start_job(b, ("v0", p))
                    for i in range(2):
                        for c in range(C):
                            t = 2 * p + i
                            last = three_passes(to[:, i * D:(i + 1) * D],
                                                lambda r: xT[:, r, c, t * P:(t + 1) * P],
                                                lambda k: wv0T[:, k, c, :], c == 0, c == C - 1)
                    last.then_inc(bank_filled, 1)

                def add_squares(h, m):
                    pe.wait_ge(squared, b * 2 * T + h * T + m + 1)
                    g = m % 4
                    mm(PS[g * HD:(g + 1) * HD, SUMS], ones[:], sq[:, m % 2],
                       start=(m < 4), stop=(m >= 4)).then_inc(sums_added, 1)

                def rel_tiles(h):
                    wait_drained(b, ("G", h, C - 1))
                    for m in range(T):
                        to = start_job(b, ("rel", h, m))
                        for c in range(C):
                            last = three_passes(to, lambda r: xT[:, r, c, m * P:(m + 1) * P],
                                                lambda k: G[:, k, c, :], c == 0, c == C - 1)
                        last.then_inc(bank_filled, 1)
                        if m >= 2:
                            add_squares(h, m - 2)

                def norm_columns(h):
                    pe.wait_ge(sums_out, b * 2 + h + 1)
                    for t in range(TH):
                        last = mm(PS[:, COLS, t:t + 1], sums[:, t * P:(t + 1) * P], pick[:],
                                  start=True, stop=True)
                    last.then_inc(cols_ready, 1)

                def out_tiles(h):
                    pe.wait_ge(rel_cut, b * 2 * T + (h + 1) * T)
                    for t in range(TH):
                        to = start_job(b, ("out", h, t))
                        for m in range(T):
                            last = three_passes(to[:, 0:D], lambda r: rel[:, r, m, t * P:(t + 1) * P],
                                                lambda k: v0[k][:, m, :], m == 0, m == T - 1)
                        last.then_inc(bank_filled, 1)
                        if t == 0:
                            norm_columns(h)

                def turn_x1(h):
                    pe.wait_ge(x1_ready, 1 + b * T + (h + 1) * TH)
                    for c in range(C):
                        to = start_job(b, ("x1T", h, c))
                        for i in range(TH):
                            last = nc.tensor.transpose(to[:, i * P:(i + 1) * P],
                                                       x1[:, h * TH + i, c * P:(c + 1) * P], ident[:])
                        last.then_inc(bank_filled, 1)
                    wait_drained(b, ("x1T", h, C - 1))

                def project_qk(h):
                    for w in range(2 * HG):
                        hg, q = divmod(w, 2)
                        to = start_job(b, ("qk", h, w))
                        for c in range(C):
                            last = mm(to, (wq if q else wk)[:, c, hg * P:(hg + 1) * P],
                                      x1T[:, c, h * HALF:(h + 1) * HALF], start=(c == 0), stop=(c == C - 1))
                        last.then_inc(bank_filled, 1)

                def values(h):
                    for p in range(TH // 2):
                        to = start_job(b, ("v1", h, p))
                        for i in range(2):
                            t = h * TH + 2 * p + i
                            for c in range(C):
                                last = mm(to[:, i * D:(i + 1) * D], x1T[:, c, t * P:(t + 1) * P], wv[:, c, :],
                                          start=(c == 0), stop=(c == C - 1))
                        last.then_inc(bank_filled, 1)

                rel_tiles(0)
                project_g(1)
                add_squares(0, T - 2)
                add_squares(0, T - 1)
                wait_drained(b, ("v0", T // 2 - 1))
                out_tiles(0)
                rel_tiles(1)
                turn_x1(0)
                project_qk(0)
                add_squares(1, T - 2)
                add_squares(1, T - 1)
                out_tiles(1)
                values(0)
                turn_x1(1)
                project_qk(1)
                values(1)

                def score(u):
                    g, hg, q0, qi, j = unit(u)
                    if u >= 2:
                        pe.wait_ge(masked, b * UNITS + u - 1)
                    if u % UPG == 0:
                        pe.wait_ge(qs_in[g % 2], (b * (GROUPS // 2) + g // 2 + 1) * 16 * 4 * HPG)
                    if u % (UNITS // HG) == 0:
                        pe.wait_ge(ks_in[hg], (b + 1) * K_LOADS)
                    for h in range(2):
                        last = mm(PS[:, 2 * (u % 2) + h], QS[:, g % 2, j, qi * P:(qi + 1) * P].bitcast(F32R),
                                  (KS1 if hg else KS0)[:, j, h * HALF:(h + 1) * HALF].bitcast(F32R),
                                  start=True, stop=True)
                    last.then_inc(scores, 1)

                def turn(u):
                    pe.wait_ge(probs, b * UNITS + u + 1)
                    for k, (free, done) in enumerate(((pt_a, turned_a), (pt_b, turned_b))):
                        pe.wait_ge(free, 1 + b * UNITS + u)
                        for i in range(TH):
                            t = k * TH + i
                            last = nc.tensor.transpose(PS[:, 4 + k, i * P:(i + 1) * P],
                                                       nr[:, u % NRING, t * P:(t + 1) * P], ident[:])
                        last.then_inc(done, 1)

                def outputs(g, t):
                    hg = unit(g * UPG)[1]
                    if t == 0:
                        pe.wait_ge(pt_a, 1 + b * UNITS + (g + 1) * UPG)
                        pe.wait_ge(pt_b, 1 + b * UNITS + (g + 1) * UPG)
                        pe.wait_ge(o_ready, 1 + b * GROUPS + g)
                    for j in range(HPG):
                        h = hg * HPG + j
                        last = mm(PS[j * HD:(j + 1) * HD, SUMS, 0:GQ], vs[:, t, h * HD:(h + 1) * HD],
                                  pt[:, g % 2, j, t, :], start=(t == 0), stop=(t == T - 1))
                    if t == T - 1:
                        last.then_inc(pv_done, 1)

                def turn_rowsums(g):
                    pe.wait_ge(rexp_ready, b * GROUPS + g + 1)
                    pe.wait_ge(rT_ready, 1 + b * GROUPS + g)
                    for qi in range(QT):
                        last = nc.tensor.transpose(PS[:, COLS, qi * P:(qi + 1) * P],
                                                   rexp[:, qi].rearrange("p j d -> p (j d)"), ident[:])
                    last.then_inc(rT_filled, 1)

                def project_out(p):
                    pe.wait_ge(o_ready, 1 + b * GROUPS + GROUPS // 2 + p + 1)
                    for i in range(2):
                        t = 2 * p + i
                        for c in range(C):
                            last = mm(PS[:, WO_BANK[p], i * D:(i + 1) * D], QO[:, c, t * P:(t + 1) * P],
                                      wo[:, c, :], start=(c == 0), stop=(c == C - 1))
                    last.then_inc(wo_filled, 1)

                wait_drained(b, ("qk", 1, 2 * HG - 1))
                wait_drained(b, ("v1", 1, TH // 2 - 1))
                score(0)
                score(1)
                for u in range(UNITS):
                    g, r = divmod(u, UPG)
                    if u + 2 < UNITS:
                        score(u + 2)
                    if g >= 6 and r == 1:
                        project_out(g - 6)
                    turn(u)
                    if g >= 1:
                        if r == 4:
                            if g >= 6:
                                pe.wait_ge(wo_drained, 1 + b * (T // 2) + g - 5)
                            turn_rowsums(g - 1)
                        outputs(g - 1, r)
                pe.wait_ge(wo_drained, 1 + b * (T // 2) + 2)
                turn_rowsums(GROUPS - 1)
                for t in range(T):
                    outputs(GROUPS - 1, t)
                project_out(2)
                project_out(3)

        @block.scalar
        def _(act):
            for s in (act_drained, pt_a, rT_ready):
                act.sem_inc(s, 1)
            act.wait_ge(setup_pe, 2 * C * C)
            for m in range(C):
                act.activation(A0[:, 0, m, :], PS[:, m, 0:D], ACT.Copy).then_inc(setup_high, 1)
                act.activation(wv0T[:, 0, m, :], PS[:, 2 + m, 0:D], ACT.Copy).then_inc(setup_high, 1)

            with act.Fori(0, B) as b:
                def fill_wait(name):
                    act.wait_ge(bank_filled, b * len(JOBS) + filled(name))
                    return PS[:, bank(name)]

                def high_half(dst, name):
                    act.activation(dst, fill_wait(name), ACT.Copy).then_inc(high, 1)

                for q in range(2):
                    for c in range(C):
                        high_half(xT[:, 0, c, q * HALF:(q + 1) * HALF], ("xT", c, q))
                for m in range(C):
                    high_half(G[:, 0, m, :], ("G", 0, m))
                for p in range(T // 2):
                    high_half(v0h[:, 2 * p:2 * p + 2, :].rearrange("p t d -> p (t d)"), ("v0", p))

                def rel_high(h):
                    for m in range(T):
                        i = h * T + m
                        act.wait_ge(dve_drained, 1 + b * DRAINS["dve"] + drained(("rel", h, m))[1])
                        act.activation(rel[:, 0, m, :], rf[:, i % 2], ACT.Copy).then_inc(high, 1)
                        if i >= 2:
                            act.wait_ge(sums_added, b * 2 * T + i - 1)
                        act.activation(sq[:, i % 2], rf[:, i % 2], ACT.Square).then_inc(squared, 1)

                def move_sums(h):
                    act.wait_ge(sums_added, b * 2 * T + (h + 1) * T)
                    if h:
                        act.wait_ge(cols_ready, b * 2 + h)
                    act.activation(sums[:], PS[:, SUMS], ACT.Copy).then_inc(sums_out, 1)

                def drain_project(h):
                    for c in range(C):
                        act.activation(x1T[:, c, h * HALF:(h + 1) * HALF], fill_wait(("x1T", h, c)),
                                       ACT.Copy).then_inc(act_drained, 1)
                    for w in range(2 * HG):
                        hg, q = divmod(w, 2)
                        n = h * 2 * HG + w
                        if n == 0:
                            act.wait_ge(rel_cut, (b + 1) * 2 * T)
                        if n >= 2:
                            act.wait_ge(lo_ready, b * 4 * HG + n - 1)
                        act.activation(rf[:, n % 2], fill_wait(("qk", h, w)), ACT.Identity,
                                       bias=(bqc if q else bkc)[:, hg:hg + 1],
                                       scale=QSCALE if q else 1.0).then_inc(act_drained, 1)
                        act.wait_ge(act_drained, 1 + b * DRAINS["act"] + drained(("qk", h, w))[1])
                        dst = qhi[:, hg] if q else (k1 if hg else k0)[:, 0]
                        act.activation(dst[:, h * HALF:(h + 1) * HALF].bitcast(F32R), rf[:, n % 2],
                                       ACT.Copy).then_inc(hi_ready, 1)

                rel_high(0)
                for m in range(C):
                    high_half(G[:, 0, m, :], ("G", 1, m))
                move_sums(0)
                rel_high(1)
                drain_project(0)
                move_sums(1)
                drain_project(1)

                def exps(u):
                    act.wait_ge(masked, b * UNITS + u + 1)
                    act.activation(nr[:, u % NRING], nr[:, u % NRING], ACT.Exp, bias=least[:, u:u + 1],
                                   scale=-1.0, accum_out=rowsum[:, u:u + 1]).then_inc(probs, 1)

                def rowsums_out(g):
                    act.wait_ge(rT_filled, 1 + b * GROUPS + g + 1)
                    act.wait_ge(o_ready, 1 + b * GROUPS + g)
                    act.activation(rT[:], PS[:, COLS, 0:GQ], ACT.Copy).then_inc(rT_ready, 1)

                exps(0)
                exps(1)
                for u in range(UNITS):
                    g, r = divmod(u, UPG)
                    _, _, _, qi, j = unit(u)
                    if u == UPG:
                        act.wait_ge(ks_in[1], (b + 1) * K_LOADS)
                    if r == 0 and g >= 2:
                        act.wait_ge(pv_done, 1 + b * GROUPS + g - 1)
                    act.wait_ge(turned_a, b * UNITS + u + 1)
                    act.activation(pt[:, g % 2, j, 0:TH, qi * P:(qi + 1) * P],
                                   PS[:, 4].rearrange("p (t q) -> p t q", q=P), ACT.Copy).then_inc(pt_a, 1)
                    if u + 2 < UNITS:
                        exps(u + 2)
                    if g >= 1 and r == 6:
                        rowsums_out(g - 1)
                rowsums_out(GROUPS - 1)

        @block.vector
        def _(dve):
            v = nc.vector
            for s in (dve_drained, pt_b, o_ready, x1_ready, wo_drained):
                dve.sem_inc(s, 1)
            dve.sem_inc(out_done, 16)
            dve.wait_ge(w_in, 16 * 14)
            v.tensor_scalar(negmask[:], negmask[:], 1.0, -MASK, ALU.subtract, ALU.mult).then_inc(mask_ready, 1)
            v.tensor_scalar(bqc[:], bqc[:], QSCALE, None, ALU.mult).then_inc(setup_dve, 1)
            dve.wait_ge(setup_high, 2 * C)
            for m in range(C):
                v.tensor_tensor(A0[:, 1, m, :], PS[:, m, 0:D], A0[:, 0, m, :].bitcast(F32),
                                ALU.subtract).then_inc(setup_dve, 1)
                v.tensor_tensor(wv0T[:, 1, m, :], PS[:, 2 + m, 0:D], wv0T[:, 0, m, :].bitcast(F32),
                                ALU.subtract).then_inc(setup_dve, 1)

            with dve.Fori(0, B) as b:
                def fill_wait(name):
                    dve.wait_ge(bank_filled, b * len(JOBS) + filled(name))
                    return PS[:, bank(name)]

                def low_half(dst, hi, name):
                    dve.wait_ge(high, b * len(CUT) + cut_high(name))
                    v.tensor_tensor(dst, PS[:, bank(name)], hi.bitcast(F32), ALU.subtract) \
                        .then_inc(dve_drained, 1)

                for q in range(2):
                    for c in range(C):
                        cols = slice(q * HALF, (q + 1) * HALF)
                        low_half(xT[:, 1, c, cols], xT[:, 0, c, cols], ("xT", c, q))
                for m in range(C):
                    low_half(G[:, 1, m, :], G[:, 0, m, :], ("G", 0, m))
                for p in range(T // 2):
                    pair = [w[:, 2 * p:2 * p + 2, :].rearrange("p t d -> p (t d)") for w in v0]
                    low_half(pair[1], pair[0], ("v0", p))

                def mask_rel(h):
                    def cut_rel(m):
                        i = h * T + m
                        dve.wait_ge(high, b * len(CUT) + cut_high(("rel", h, m)))
                        v.tensor_tensor(rel[:, 1, m, :], rf[:, i % 2], rel[:, 0, m, :].bitcast(F32),
                                        ALU.subtract).then_inc(rel_cut, 1)

                    for m in range(T):
                        i = h * T + m
                        dve.wait_ge(adj_in[i % ADJ], (b * (2 * T // ADJ) + i // ADJ + 1) * 16)
                        if i >= 2:
                            dve.wait_ge(squared, b * 2 * T + i - 1)
                            dve.wait_ge(rel_cut, b * 2 * T + i - 1)
                        v.tensor_tensor(rf[:, i % 2], fill_wait(("rel", h, m)), adjr[:, i % ADJ], ALU.mult) \
                            .then_inc(dve_drained, 1)
                        if m >= 1:
                            cut_rel(m - 1)
                    cut_rel(T - 1)

                def norm_out(h):
                    dve.wait_ge(cols_ready, b * 2 + h + 1)
                    v.tensor_copy(nsq[:, h * TH:(h + 1) * TH], PS[:, COLS, 0:TH]).then_inc(nsq_ready, 1)

                def residual(h):
                    dve.wait_ge(rnorm_ready, b * 2 + h + 1)
                    if h == 0:
                        dve.wait_ge(out_done, 16 + b * 16)
                    for i in range(TH):
                        t = h * TH + i
                        v.scalar_tensor_tensor(out=x1[:, t], in0=fill_wait(("out", h, i))[:, 0:D],
                                               scalar=rnorm[:, t:t + 1], in1=xs[:, t], op0=ALU.mult,
                                               op1=ALU.add).then_inc(dve_drained, 1)
                        dve.wait_ge(dve_drained, 1 + b * DRAINS["dve"] + drained(("out", h, i))[1])
                        v.bn_stats(stats[:, t], x1[:, t]).then_inc(stat_step, 1)
                    alone(dve, stat_step, b * 2 * T + (h + 1) * TH)
                    for i in range(TH):
                        t = h * TH + i
                        last = v.bn_aggr(mv[:, t], stats[:, t])
                    last.then_inc(var_ready, 1)
                    dve.wait_ge(rstd_ready, b * 2 + h + 1)
                    for i in range(TH):
                        t = h * TH + i
                        v.tensor_scalar(x1[:, t], x1[:, t], mv[:, t, 0:1], rstd[:, t:t + 1],
                                        ALU.subtract, ALU.mult).then_inc(x1_ready, 1)

                def cut(h):
                    for w in range(2 * HG):
                        hg, q = divmod(w, 2)
                        n = h * 2 * HG + w
                        cols = slice(h * HALF, (h + 1) * HALF)
                        kh = (k1 if hg else k0)
                        hi, lo = (qhi[:, hg], qlo[:, hg]) if q else (kh[:, 0], kh[:, 1])
                        dve.wait_ge(hi_ready, b * 4 * HG + n + 1)
                        v.tensor_tensor(lo[:, cols].bitcast(F32R), rf[:, n % 2], hi[:, cols], ALU.subtract) \
                            .then_inc(lo_ready, 1)

                def add_bv(h):
                    for p in range(TH // 2):
                        t = h * TH + 2 * p
                        src = fill_wait(("v1", h, p)).rearrange("p (t d) -> p t d", d=D)
                        v.tensor_tensor(vs[:, t:t + 2, :], src, bvb[:].rearrange("p (a d) -> p a d", a=1)
                                        .to_broadcast([P, 2, D]), ALU.add).then_inc(dve_drained, 1)

                mask_rel(0)
                for m in range(C):
                    low_half(G[:, 1, m, :], G[:, 0, m, :], ("G", 1, m))
                norm_out(0)
                residual(0)
                mask_rel(1)
                cut(0)
                norm_out(1)
                residual(1)
                add_bv(0)
                cut(1)
                add_bv(1)

                def mask_scores(u):
                    _, _, q0, qi, _ = unit(u)
                    if u >= NRING:
                        dve.wait_ge(turned_b, b * UNITS + u - NRING + 1)
                    alone(dve, scores, 1 + b * UNITS + u + 1)
                    k = 2 * (u % 2)
                    v.tensor_tensor_reduce(out=nr[:, u % NRING], in0=PS[:, k:k + 2].rearrange("p k n -> p (k n)"),
                                           in1=negmask[:, q0 // P + qi], scale=1.0, scalar=3.0e38,
                                           op0=ALU.add, op1=ALU.min,
                                           accum_out=least[:, u:u + 1]).then_inc(masked, 1)

                def group_out(g):
                    _, hg, q0, _, _ = unit(g * UPG)
                    dve.wait_ge(pv_done, 1 + b * GROUPS + g + 1)
                    dve.wait_ge(rT_ready, 1 + b * GROUPS + g + 1)
                    v.tensor_tensor(QO[:, hg, q0:q0 + GQ], PS[:, SUMS, 0:GQ], rT[:], ALU.mult) \
                        .then_inc(o_ready, 1)

                def residual_out(p):
                    if p == 0:
                        dve.wait_ge(x1b_ready, (b + 1) * T)
                    dve.wait_ge(wo_filled, b * (T // 2) + p + 1)
                    dst = x1[:, 2 * p:2 * p + 2, :].rearrange("p t d -> p (t d)")
                    v.tensor_tensor(dst, PS[:, WO_BANK[p]], dst, ALU.add).then_inc(wo_drained, 1)
                    dve.wait_ge(wo_drained, 1 + b * (T // 2) + p + 1)
                    for t in (2 * p, 2 * p + 1):
                        v.bn_stats(stats[:, t], x1[:, t]).then_inc(stat_step, 1)

                mask_scores(0)
                mask_scores(1)
                for u in range(UNITS):
                    g, r = divmod(u, UPG)
                    _, _, _, qi, j = unit(u)
                    if u + 2 < UNITS:
                        mask_scores(u + 2)
                    if u == UPG:
                        dve.wait_ge(ks_in[1], (b + 1) * K_LOADS)
                    if r == 0 and g >= 2:
                        group_out(g - 2)
                    dve.wait_ge(turned_b, b * UNITS + u + 1)
                    v.tensor_copy(pt[:, g % 2, j, TH:T, qi * P:(qi + 1) * P],
                                  PS[:, 5].rearrange("p (t q) -> p t q", q=P)).then_inc(pt_b, 1)
                    if g >= 6 and r == 2:
                        residual_out(g - 6)
                group_out(GROUPS - 2)
                group_out(GROUPS - 1)
                residual_out(2)
                residual_out(3)
                alone(dve, stat_step, (b + 1) * 2 * T)
                for t in range(T):
                    last = v.bn_aggr(mv[:, t], stats[:, t])
                last.then_inc(var_ready, 1)


_INS = ["x", "adj", "L0_gnn_Wq", "L0_gnn_Wk", "L0_gnn_Wv", "L1_gnn_Wq", "L1_gnn_bq", "L1_gnn_Wk", "L1_gnn_bk",
        "L1_gnn_Wv", "L1_gnn_bv", "L1_gnn_Wo", "L1_gnn_bo"]


def kernel(**inputs):
    import concourse.bacc as bacc
    from concourse.bass_utils import run_bass_kernel_spmd

    nc = bacc.Bacc("TRN2", target_bir_lowering=False, num_devices=1, dynamic_dma_scratch_size=2048)
    arrays, args = {}, []
    for name in _INS:
        a = np.ascontiguousarray(inputs[name])
        arrays[f"in_{name}"] = a
        args.append(nc.dram_tensor(f"in_{name}", a.shape, mybir.dt.from_np(a.dtype), kind="ExternalInput").ap())
    out = nc.dram_tensor("out_0", (B, N, D), F32, kind="ExternalOutput").ap()
    build(nc, *args, out)
    r = run_bass_kernel_spmd(nc, [arrays], core_ids=[0])
    return r.results[0]["out_0"]
```

```python
from contextlib import ExitStack

import numpy as np

import concourse.bass as bass
from concourse import mybir

ALU = mybir.AluOpType
ACT = mybir.ActivationFunctionType
F32 = mybir.dt.float32
F32R = mybir.dt.float32r

B, N, D, H = 8, 1024, 256, 8
HD = D // H
P = 128
C = D // P
T = N // P
HALF = 512
TH = HALF // P
HPG = P // HD
HG = H // HPG
GQ = 256
QT = GQ // P
UPG = QT * HPG
GROUPS = HG * (N // GQ)
UNITS = GROUPS * UPG
MASK = 1.0e9
EPS = 1e-5
QSCALE = -1.0 / float(np.sqrt(np.float32(HD)))
RING = 6
SUMS, COLS = 6, 7
WO_BANK = (COLS, COLS, 1, SUMS)
TURN_AT = 6
PARTS = 3
NRING = 3
ADJ = 4


def job_list():
    jobs = [("xT", c, q) for q in range(2) for c in range(C)]
    jobs += [("G", 0, m) for m in range(C)]
    jobs += [("v0", p) for p in range(T // 2)]
    jobs += [("rel", 0, m) for m in range(T)]
    jobs += [("G", 1, m) for m in range(C)]
    jobs += [("out", 0, t) for t in range(TH)]
    jobs += [("rel", 1, m) for m in range(TURN_AT)]
    jobs += [("x1T", 0, c) for c in range(C)]
    jobs += [("rel", 1, m) for m in range(TURN_AT, T)]
    jobs += [("qk", 0, 0), ("qk", 0, 1)]
    jobs += [("out", 1, t) for t in range(TH)]
    jobs += [("qk", 0, 2), ("v1", 0, 0)]
    jobs += [("x1T", 1, c) for c in range(C)]
    jobs += [("v1", 0, 1)]
    jobs += [("qk", 1, 0), ("qk", 1, 1), ("v1", 1, 0), ("v1", 1, 1)]
    jobs += [("qk", 1, 2), ("qk", 0, 3), ("qk", 1, 3)]
    return jobs


JOBS = job_list()
CUT = [name for name in JOBS if name[0] not in ("out", "v1")]
INDEX = {name: i for i, name in enumerate(JOBS)}
LATE = ("qk", 1, 3)
FIRST_BANK = (5 - (len(JOBS) - 2)) % RING


def bank(name):
    return SUMS if name == LATE else (INDEX[name] + FIRST_BANK) % RING


def done(name):
    return INDEX[name] + 1


def cut_high(name):
    return CUT.index(name) + 1


def act_copies_second(u):
    g, r = divmod(u, UPG)
    return r == 3 or (g == 6 and r == 2)


def out_bank(g):
    return SUMS if g < GROUPS - 1 else 2


def unit(u):
    g, r = divmod(u, UPG)
    hg, qp = divmod(g, N // GQ)
    qi, j = divmod(r, HPG)
    return g, hg, qp * GQ, qi, j


def build(nc, x, adj, wq0, wk0, wv0, wq1, bq1, wk1, bk1, wv1, bv1, wo1, bo1, out):
    with ExitStack() as ctx:
        def sb(name, shape, dt=F32):
            return ctx.enter_context(nc.sbuf_tensor(name, shape, dt))

        def sem(name):
            return ctx.enter_context(nc.semaphore(name))

        PS = ctx.enter_context(nc.psum_tensor("PS", [P, 8, HALF], F32))

        def overlay(size, *sets):
            found = []
            for one in sets:
                with ExitStack() as place:
                    for name, shape, dt in one:
                        found.append(place.enter_context(nc.sbuf_tensor(name, shape, dt)))
            sb(sets[0][0][0] + "_place", [P, size])
            return found

        negmask = sb("negmask", [P, T, N])
        A0 = sb("A0", [P, 2, C, D], F32R)
        wv0T = sb("wv0T", [P, 2, C, D], F32R)
        w1 = sb("w1", [P, 3, 2, C, D], F32R)
        wo = sb("wo", [P, C, D])
        bqc = sb("bqc", [P, C])
        bkc = sb("bkc", [P, C])
        bvb = sb("bvb", [P, D])
        bob = sb("bob", [P, D])
        ident = sb("ident", [P, P])
        ones = sb("ones", [P, HD])
        pick = sb("pick", [P, 1])
        mhalf = sb("mhalf", [P, T])
        minus = sb("minus", [P, T])
        eps = sb("eps", [P, T])
        xs, x1Tal = overlay(T * D, [("xs", [P, T, D], F32)], [("x1Tal", [P, C, HALF], F32R)])
        x1 = sb("x1", [P, T, D])
        qhi = QO = sb("QO", [P, HG, N])
        qlo = sb("qlo", [P, HG, N])
        k0 = sb("k0", [P, 2, N])
        QS = sb("QS", [P, 2, HPG, GQ])
        KS0 = sb("KS0", [P, HPG, N])
        vs, v0h = overlay(T * D, [("vs", [P, T, D], F32)], [("v0h", [P, T, D], F32R)])
        KS1, adjr, sq, rf = overlay(
            HPG * N,
            [("KS1", [P, HPG, N], F32)],
            [("adjr", [P, ADJ, HALF], F32),
             ("sq", [P, 2, HALF], F32),
             ("rf", [P, 2, HALF], F32)])
        pt, nr, rel, xT, v0l, k1, G, x1Ta, _, x1Tb = overlay(
            2 * HPG * T * GQ + NRING * N,
            [("pt", [P, 2, HPG, T, GQ], F32), ("nr", [P, NRING, N], F32)],
            [("rel", [P, 2, T, HALF], F32R),
             ("xT", [P, 2, C, N], F32R),
             ("v0l", [P, T, D], F32R),
             ("k1", [P, 2, N], F32),
             ("G", [P, 2, C, HALF], F32R),
             ("x1Ta", [P, C, HALF], F32R)],
            [("before_x1Tb", [P, 2 * T * HALF], F32), ("x1Tb", [P, 2, C, HALF], F32R)])
        stats = sb("stats", [P, T, 6])
        nsq = sb("nsq", [P, T])
        rnorm = sb("rnorm", [P, T])
        mv = sb("mv", [P, T, 2])
        rstd = sb("rstd", [P, T])
        least = sb("least", [P, UNITS])
        rowsum = sb("rowsum", [P, UNITS])
        rrow = sb("rrow", [P, UPG])
        v0 = (v0h, v0l)
        x1T = ((x1Ta[:], x1Tal[:]), (x1Tb[:, 0], x1Tb[:, 1]))
        sums = QO[:, HG - 1, HALF:N]
        rexp = k0[:, 0, 0:QT * P].rearrange("p (q j d) -> p q j d", q=QT, j=HPG)
        rT = k0[:, 1, 0:GQ]
        w0, w1in = [pt[:, 0, k, 0:6].rearrange("p (w c) d -> p w c d", c=C) for k in range(2)]

        passed = sem("passed")
        w0_in = sem("w0_in")
        w1_in = sem("w1_in")
        wo_in = sem("wo_in")
        mask_in = [sem(f"mask_in{k}") for k in range(2)]
        stacks_ready = sem("stacks_ready")
        consts = sem("consts")
        setup_pe = sem("setup_pe")
        setup_high = sem("setup_high")
        setup_dve = sem("setup_dve")
        w1_high = sem("w1_high")
        w1_low = sem("w1_low")
        mask_ready = sem("mask_ready")
        x_in = sem("x_in")
        adj_in = [sem(f"adj_in{k}") for k in range(ADJ)]
        bank_filled = sem("bank_filled")
        high = sem("high")
        drained = sem("drained")
        rel_cut = sem("rel_cut")
        squared = sem("squared")
        sums_added = sem("sums_added")
        sums_out = sem("sums_out")
        cols_ready = sem("cols_ready")
        nsq_ready = sem("nsq_ready")
        rnorm_ready = sem("rnorm_ready")
        stat_step = sem("stat_step")
        var_ready = sem("var_ready")
        pool_step = sem("pool_step")
        rstd_ready = sem("rstd_ready")
        x1_ready = sem("x1_ready")
        x1b_ready = sem("x1b_ready")
        q_scaled = sem("q_scaled")
        ks_in = [[sem(f"ks_in{g}{j}") for j in range(HPG)] for g in range(HG)]
        qs_in = [[sem(f"qs_in{g}{j}") for j in range(HPG)] for g in range(2)]
        scores = sem("scores")
        masked = sem("masked")
        probs = sem("probs")
        turned_a = sem("turned_a")
        turned_b = sem("turned_b")
        pt_a = sem("pt_a")
        pt_b = sem("pt_b")
        rrow_ready = sem("rrow_ready")
        rexp_ready = sem("rexp_ready")
        rT_filled = sem("rT_filled")
        rT_ready = sem("rT_ready")
        pv_done = sem("pv_done")
        o_ready = sem("o_ready")
        wo_filled = sem("wo_filled")
        wo_drained = sem("wo_drained")
        y_ready = sem("y_ready")
        out_done = sem("out_done")

        block = ctx.enter_context(nc.Block())
        xv = x.rearrange("b (t p) d -> b p t d", p=P)
        ov = out.rearrange("b (t p) d -> b p t d", p=P)
        adjv = adj.rearrange("(t p) n -> p t n", p=P)
        wview = lambda w: w.rearrange("(c p) e -> p c e", p=P)
        row = lambda v: v.rearrange("(a n) -> a n", a=1)
        K_LOADS = (32 * PARTS, 32 * HPG)
        Q_LOADS = 16 * PARTS
        VARS = 3 + T // 2

        def alone(eng, signal, value):
            eng.wait_ge(signal, value)
            eng.sem_inc(passed, 1)

        def load_x(sp, b):
            sp.dma_start(xs[:], xv[bass.ds(b, 1)].rearrange("o p t d -> p (o t) d")).then_inc(x_in, 16)

        def load_adj(sp, i):
            h, m = divmod(i, T)
            sp.dma_start(adjr[:, i % ADJ], adjv[:, m, h * HALF:(h + 1) * HALF]).then_inc(adj_in[i % ADJ], 16)

        def load_k(sp, hg, cols, inc):
            for j in range(HPG):
                for r in range(HPG if hg else PARTS):
                    sp.dma_start((KS1 if hg else KS0)[r * HD:(r + 1) * HD, j, cols],
                                 (k1 if hg else k0)[j * HD:(j + 1) * HD, r % 2, cols]).then_inc(ks_in[hg][j], inc)

        def load_q(sp, g):
            _, hg, q0, _, _ = unit(g * UPG)
            for j in range(HPG):
                for r, src in enumerate((qhi, qhi, qlo)):
                    sp.dma_start(QS[r * HD:(r + 1) * HD, g % 2, j, :],
                                 src[j * HD:(j + 1) * HD, hg, q0:q0 + GQ]).then_inc(qs_in[g % 2][j], 16)

        def load_first_q(sp):
            for j in range(HPG):
                for r, src in enumerate((qhi, qhi, qlo)):
                    sp.dma_start(QS[r * HD:(r + 1) * HD, :, j, :],
                                 src[j * HD:(j + 1) * HD, 0, 0:2 * GQ].rearrange("p (g q) -> p g q", g=2)) \
                      .then_inc(qs_in[0][j], 16)

        @block.sync
        def _(sp):
            for w, src in enumerate((wq0, wk0, wv0)):
                sp.dma_start(w0[:, w], wview(src)).then_inc(w0_in, 16)
            for w, src in enumerate((wq1, wk1, wv1)):
                sp.dma_start(w1in[:, w], wview(src)).then_inc(w1_in, 16)
            for dst, src in ((bqc, bq1), (bkc, bk1)):
                for c in range(C):
                    sp.dma_start(dst[:, c:c + 1], src[c * P:(c + 1) * P].rearrange("(p a) -> p a", a=1)) \
                      .then_inc(w1_in, 16)
            load_x(sp, 0)
            for k in range(2):
                tiles = slice(k * TH, (k + 1) * TH)
                sp.dma_start(negmask[:, tiles], adjv[:, tiles]).then_inc(mask_in[k], 16)
            sp.dma_start(wo[:], wview(wo1)).then_inc(wo_in, 16)
            for dst, src in ((bvb, bv1), (bob, bo1)):
                sp.dma_start(dst[:], row(src).to_broadcast([P, D])).then_inc(wo_in, 16)
            for i in range(ADJ):
                load_adj(sp, i)
            with sp.Fori(0, B) as b:
                for i in range(ADJ, 2 * T):
                    h0, m0 = divmod(i - ADJ, T)
                    sp.wait_ge(drained, 1 + b * len(JOBS) + done(("rel", h0, m0)))
                    load_adj(sp, i)
                first, second = slice(0, HALF), slice(HALF, N)
                sp.wait_ge(drained, 1 + b * len(JOBS) + done(("qk", 0, 0)))
                load_k(sp, 0, first, 16)
                sp.wait_ge(drained, 1 + b * len(JOBS) + done(("qk", 0, 1)))
                load_first_q(sp)
                sp.wait_ge(drained, 1 + b * len(JOBS) + done(("qk", 1, 0)))
                load_k(sp, 0, second, 16)
                sp.wait_ge(drained, 1 + b * len(JOBS) + done(("qk", 1, 2)))
                load_k(sp, 1, slice(0, N), 32)
                sp.wait_ge(drained, 1 + (b + 1) * len(JOBS))
                load_x(sp, (b + 1) % B)
                for g in range(2, GROUPS):
                    sp.wait_ge(scores, 1 + b * UNITS + (g - 1) * UPG)
                    load_q(sp, g)
                sp.wait_ge(scores, 1 + (b + 1) * UNITS)
                for i in range(ADJ):
                    load_adj(sp, i)
                for h in range(2):
                    sp.wait_ge(y_ready, b * T + (h + 1) * TH)
                    tiles = slice(h * TH, (h + 1) * TH)
                    sp.dma_start(ov[bass.ds(b, 1), :, tiles].rearrange("o p t d -> p (o t) d"), x1[:, tiles]) \
                      .then_inc(out_done, 16)
            sp.wait_ge(x_in, (B + 1) * 16)
            for k in range(ADJ):
                sp.wait_ge(adj_in[k], (B * (2 * T // ADJ) + 1) * 16)
            sp.wait_ge(out_done, 16 + B * 32)

        def inverse_deviation(pool, b, k, tiles, steps):
            pool.wait_ge(var_ready, b * VARS + k + 1)
            pool.tensor_tensor(rstd[:, tiles], mv[:, tiles, 1], eps[:, tiles], ALU.add).then_inc(pool_step, 1)
            pool.wait_ge(pool_step, steps + 1)
            return pool.tensor_tensor(rstd[:, tiles], rstd[:, tiles], mhalf[:, tiles], ALU.pow)

        @block.gpsimd
        def _(pool):
            pool.memset(ident[:], 0.0).then_inc(pool_step, 1)
            pool.memset(pick[:], 0.0).then_inc(pool_step, 1)
            for dst, value in ((ones, 1.0), (mhalf, -0.5), (eps, EPS), (minus, -1.0)):
                pool.memset(dst[:], value).then_inc(consts, 1)
            pool.wait_ge(pool_step, 2)
            pool.affine_select(out=ident[:], in_=ident[:], compare_op=ALU.not_equal, fill=1.0, base=0,
                               pattern=[[-1, P]], channel_multiplier=1).then_inc(consts, 1)
            for g in range(HPG):
                pool.affine_select(out=pick[:], in_=pick[:], compare_op=ALU.not_equal, fill=1.0,
                                   base=-g * HD, pattern=[[0, 1]], channel_multiplier=1).then_inc(pool_step, 1)
                pool.wait_ge(pool_step, 3 + g)
            pool.memset(rnorm[:], 0.0).then_inc(consts, 1)
            pool.wait_ge(mask_in[1], 16)
            for t in range(TH, T):
                pool.tensor_scalar(negmask[:, t], negmask[:, t], 1.0, -MASK, ALU.subtract, ALU.mult) \
                    .then_inc(mask_ready, 1)
            first = 2 + HPG
            per = 3 + 2 * (T // 2)

            with pool.Fori(0, B) as b:
                for h in range(2):
                    tiles = slice(h * TH, (h + 1) * TH)
                    pool.wait_ge(nsq_ready, b * 2 + h + 1)
                    pool.tensor_tensor(rnorm[:, tiles], nsq[:, tiles], mhalf[:, tiles], ALU.pow) \
                        .then_inc(rnorm_ready, 1)
                    for k, part in enumerate((tiles,) if h == 0 else (slice(TH, T - 1), slice(T - 1, T))):
                        inverse_deviation(pool, b, h + k, part, first + b * per + h + k).then_inc(rstd_ready, 1)
                    if h == 0:
                        alone(pool, rstd_ready, b * 3 + 1)
                        for t in range(2):
                            pool.tensor_scalar(x1[:, t], x1[:, t], mv[:, t, 0:1], rstd[:, t:t + 1],
                                               ALU.subtract, ALU.mult).then_inc(x1_ready, 1)
                pool.wait_ge(wo_in, 16 * 3)
                for h in range(2):
                    for t in range(h * TH, (h + 1) * TH):
                        if t == h * TH:
                            pool.wait_ge(bank_filled, b * len(JOBS) + done(("x1T", h, C - 1)))
                        pool.tensor_tensor(x1[:, t], x1[:, t], bob[:], ALU.add).then_inc(x1b_ready, 1)

                def normalise_out(p):
                    steps = first + b * per + 3 + 2 * p
                    inverse_deviation(pool, b, 3 + p, slice(2 * p, 2 * p + 2), steps).then_inc(pool_step, 1)
                    alone(pool, pool_step, steps + 2)
                    for t in (2 * p, 2 * p + 1):
                        pool.tensor_scalar(x1[:, t], x1[:, t], mv[:, t, 0:1], rstd[:, t:t + 1],
                                           ALU.subtract, ALU.mult).then_inc(y_ready, 1)

                for g in range(GROUPS):
                    if g == GROUPS - 1:
                        normalise_out(0)
                    pool.wait_ge(probs, b * UNITS + (g + 1) * UPG)
                    pool.tensor_tensor(rrow[:], rowsum[:, g * UPG:(g + 1) * UPG], minus[:], ALU.pow) \
                        .then_inc(rrow_ready, 1)
                    alone(pool, rT_filled, 1 + b * GROUPS + g)
                    alone(pool, rrow_ready, b * GROUPS + g + 1)
                    pool.tensor_copy(rexp, rrow[:].rearrange("p (q j a) -> p q j a", q=QT, a=1)
                                     .to_broadcast([P, QT, HPG, HD])).then_inc(rexp_ready, 1)
                for p in range(1, T // 2):
                    normalise_out(p)

        @block.tensor
        def _(pe):
            mm = nc.tensor.matmul
            for s in (pv_done, scores, rT_filled):
                pe.sem_inc(s, 1)

            def wait_drained(b, name):
                pe.wait_ge(drained, 1 + b * len(JOBS) + done(name))

            def start_job(b, name):
                i = INDEX[name]
                if i >= RING and name != LATE:
                    wait_drained(b, JOBS[i - RING])
                return PS[:, bank(name)]

            def three_passes(to, stationary, moving, first, final):
                for n, (r, k) in enumerate(((0, 0), (0, 1), (1, 0))):
                    last = mm(to, stationary(r), moving(k), start=first and n == 0, stop=final and n == 2)
                return last

            pe.wait_ge(consts, 6)
            pe.wait_ge(w0_in, 16 * 3)
            for m in range(C):
                for c in range(C):
                    mm(PS[:, m, 0:D], w0[:, 0, c, m * P:(m + 1) * P], w0[:, 1, c, :],
                       start=(c == 0), stop=(c == C - 1)).then_inc(setup_pe, 1)
                    nc.tensor.transpose(PS[:, 2 + m, c * P:(c + 1) * P], w0[:, 2, c, m * P:(m + 1) * P],
                                        ident[:]).then_inc(setup_pe, 1)
            pe.wait_ge(setup_dve, 2 * C)

            with pe.Fori(0, B) as b:
                pe.wait_ge(x_in, b * 16 + 16)
                for q in range(2):
                    for c in range(C):
                        to = start_job(b, ("xT", c, q))
                        for i in range(TH):
                            last = nc.tensor.transpose(to[:, i * P:(i + 1) * P],
                                                       xs[:, q * TH + i, c * P:(c + 1) * P], ident[:])
                        last.then_inc(bank_filled, 1)

                def project_g(h):
                    cols = slice(h * HALF, (h + 1) * HALF)
                    to = [start_job(b, ("G", h, m)) for m in range(C)]
                    for k in range(2):
                        for c in range(C):
                            if h == 0 and k == 1:
                                wait_drained(b, ("xT", c, 0))
                            for m in range(C):
                                for r in range(2 - k):
                                    last = mm(to[m], A0[:, r, c, m * P:(m + 1) * P], xT[:, k, c, cols],
                                              start=(k == c == r == 0), stop=(k == 1 and c == C - 1))
                                if k == 1 and c == C - 1:
                                    last.then_inc(bank_filled, 1)

                pe.wait_ge(high, b * len(CUT) + cut_high(("xT", C - 1, 0)))
                pe.wait_ge(wo_drained, 1 + b * (T // 2))
                project_g(0)
                wait_drained(b, ("xT", C - 1, 1))
                for p in range(T // 2):
                    to = start_job(b, ("v0", p))
                    for i in range(2):
                        for c in range(C):
                            t = 2 * p + i
                            last = three_passes(to[:, i * D:(i + 1) * D],
                                                lambda r: xT[:, r, c, t * P:(t + 1) * P],
                                                lambda k: wv0T[:, k, c, :], c == 0, c == C - 1)
                    last.then_inc(bank_filled, 1)

                def add_squares(h, m):
                    pe.wait_ge(squared, b * 2 * T + h * T + m + 1)
                    g = m % 4
                    mm(PS[g * HD:(g + 1) * HD, SUMS], ones[:], sq[:, m % 2],
                       start=(m < 4), stop=(m >= 4)).then_inc(sums_added, 1)

                def rel_tiles(h, tiles):
                    if tiles[0] == 0:
                        wait_drained(b, ("G", h, C - 1))
                    for m in tiles:
                        to = start_job(b, ("rel", h, m))
                        for c in range(C):
                            last = three_passes(to, lambda r: xT[:, r, c, m * P:(m + 1) * P],
                                                lambda k: G[:, k, c, :], c == 0, c == C - 1)
                        last.then_inc(bank_filled, 1)
                        if m >= 2:
                            add_squares(h, m - 2)

                def norm_columns(h):
                    pe.wait_ge(sums_out, b * 2 + h + 1)
                    for t in range(TH):
                        last = mm(PS[:, COLS, t:t + 1], sums[:, t * P:(t + 1) * P], pick[:],
                                  start=True, stop=True)
                    last.then_inc(cols_ready, 1)

                def out_tiles(h):
                    pe.wait_ge(rel_cut, b * 2 * T + (h + 1) * T)
                    for t in range(TH):
                        to = start_job(b, ("out", h, t))
                        for m in range(T):
                            last = three_passes(to[:, 0:D], lambda r: rel[:, r, m, t * P:(t + 1) * P],
                                                lambda k: v0[k][:, m, :], m == 0, m == T - 1)
                        last.then_inc(bank_filled, 1)
                        if t == 0:
                            norm_columns(h)

                def turn_x1(h):
                    pe.wait_ge(x1_ready, 1 + b * T + (h + 1) * TH)
                    for c in range(C):
                        to = start_job(b, ("x1T", h, c))
                        for i in range(TH):
                            last = nc.tensor.transpose(to[:, i * P:(i + 1) * P],
                                                       x1[:, h * TH + i, c * P:(c + 1) * P], ident[:])
                        last.then_inc(bank_filled, 1)

                def project_qk(h, parts):
                    for w in parts:
                        hg, q = divmod(w, 2)
                        to = start_job(b, ("qk", h, w))
                        for k in range(2):
                            if w == 0:
                                if k:
                                    wait_drained(b, ("x1T", h, C - 1))
                                else:
                                    pe.wait_ge(high, b * len(CUT) + cut_high(("x1T", h, C - 1)))
                            for c in range(C):
                                for r in range(2 - k):
                                    last = mm(to, w1[:, 0 if q else 1, r, c, hg * P:(hg + 1) * P],
                                              x1T[h][k][:, c, :], start=(k == c == r == 0),
                                              stop=(k == 1 and c == C - 1))
                        last.then_inc(bank_filled, 1)

                def values(h, pairs):
                    for p in pairs:
                        to = start_job(b, ("v1", h, p))
                        for i in range(2):
                            t = 2 * p + i
                            for c in range(C):
                                last = three_passes(to[:, i * D:(i + 1) * D],
                                                    lambda r: x1T[h][r][:, c, t * P:(t + 1) * P],
                                                    lambda k: w1[:, 2, k, c, :], c == 0, c == C - 1)
                        last.then_inc(bank_filled, 1)

                rel_tiles(0, range(T))
                project_g(1)
                add_squares(0, T - 2)
                add_squares(0, T - 1)
                wait_drained(b, ("v0", T // 2 - 1))
                out_tiles(0)
                rel_tiles(1, range(TURN_AT))
                turn_x1(0)
                rel_tiles(1, range(TURN_AT, T))
                pe.wait_ge(w1_high, 3)
                pe.wait_ge(w1_low, 3)
                project_qk(0, (0, 1))
                add_squares(1, T - 2)
                add_squares(1, T - 1)
                out_tiles(1)
                project_qk(0, (2,))
                values(0, (0,))
                turn_x1(1)
                values(0, (1,))
                project_qk(1, (0, 1))
                values(1, (0, 1))
                project_qk(1, (2,))
                project_qk(0, (3,))

                def score(u):
                    g, hg, q0, qi, j = unit(u)
                    if u >= 2:
                        pe.wait_ge(masked, b * UNITS + u - 1)
                    if qi == 0 and g % 2 == 0:
                        pe.wait_ge(qs_in[0][j], (b * (GROUPS // 2) + g // 2 + 1) * Q_LOADS)
                    if qi == 0 and g % 2 == 1 and g > 1:
                        pe.wait_ge(qs_in[1][j], (b * (GROUPS // 2 - 1) + g // 2) * Q_LOADS)
                    if qi == 0 and q0 == 0:
                        pe.wait_ge(ks_in[hg][j], (b + 1) * K_LOADS[hg])
                    for h in range(2):
                        last = mm(PS[:, 2 * (u % 2) + h], QS[:, g % 2, j, qi * P:(qi + 1) * P].bitcast(F32R),
                                  (KS1 if hg else KS0)[:, j, h * HALF:(h + 1) * HALF].bitcast(F32R),
                                  start=True, stop=True)
                    last.then_inc(scores, 1)

                def turn(u):
                    pe.wait_ge(probs, b * UNITS + u + 1)
                    for k, (free, done) in enumerate(((pt_a, turned_a), (pt_b, turned_b))):
                        pe.wait_ge(free, 1 + b * UNITS + u)
                        for i in range(TH):
                            t = k * TH + i
                            last = nc.tensor.transpose(PS[:, 4 + k, i * P:(i + 1) * P],
                                                       nr[:, u % NRING, t * P:(t + 1) * P], ident[:])
                        last.then_inc(done, 1)

                def outputs(g, t):
                    hg = unit(g * UPG)[1]
                    if t == 0:
                        pe.wait_ge(pt_a, 1 + b * UNITS + (g + 1) * UPG)
                        pe.wait_ge(pt_b, 1 + b * UNITS + (g + 1) * UPG)
                        if g < GROUPS - 1:
                            pe.wait_ge(o_ready, 1 + b * GROUPS + g)
                    for j in range(HPG):
                        h = hg * HPG + j
                        last = mm(PS[j * HD:(j + 1) * HD, out_bank(g), 0:GQ], vs[:, t, h * HD:(h + 1) * HD],
                                  pt[:, g % 2, j, t, :], start=(t == 0), stop=(t == T - 1))
                    if t == T - 1:
                        last.then_inc(pv_done, 1)

                def turn_rowsums(g):
                    pe.wait_ge(rexp_ready, b * GROUPS + g + 1)
                    pe.wait_ge(rT_ready, 1 + b * GROUPS + g)
                    for qi in range(QT):
                        last = nc.tensor.transpose(PS[:, COLS, qi * P:(qi + 1) * P],
                                                   rexp[:, qi].rearrange("p j d -> p (j d)"), ident[:])
                    last.then_inc(rT_filled, 1)

                def project_out(p):
                    if p == 0:
                        pe.wait_ge(wo_in, 16 * 3)
                    pe.wait_ge(o_ready, 1 + b * GROUPS + GROUPS // 2 + p + 1)
                    for i in range(2):
                        t = 2 * p + i
                        for c in range(C):
                            last = mm(PS[:, WO_BANK[p], i * D:(i + 1) * D], QO[:, c, t * P:(t + 1) * P],
                                      wo[:, c, :], start=(c == 0), stop=(c == C - 1))
                    last.then_inc(wo_filled, 1)

                pe.wait_ge(stacks_ready, 2)
                wait_drained(b, ("qk", 1, 1))
                score(0)
                wait_drained(b, ("v1", 1, 1))
                score(1)
                project_qk(1, (3,))
                wait_drained(b, ("qk", 0, 3))
                for u in range(UNITS):
                    g, r = divmod(u, UPG)
                    if u + 2 < UNITS:
                        score(u + 2)
                    if g == 6 and r == 1:
                        project_out(0)
                    turn(u)
                    if g >= 1:
                        if r == 4:
                            if g == 6:
                                pe.wait_ge(wo_drained, 1 + b * (T // 2) + 1)
                            turn_rowsums(g - 1)
                        outputs(g - 1, r)
                pe.wait_ge(rT_ready, b * GROUPS + GROUPS)
                project_out(1)
                for t in range(T):
                    if t == TH:
                        pe.wait_ge(wo_drained, 1 + b * (T // 2) + 2)
                        turn_rowsums(GROUPS - 1)
                    outputs(GROUPS - 1, t)
                project_out(2)
                project_out(3)

        @block.scalar
        def _(act):
            for s in (pt_a, rT_ready):
                act.sem_inc(s, 1)
            act.wait_ge(setup_pe, 2 * C * C)
            for m in range(C):
                act.activation(A0[:, 0, m, :], PS[:, m, 0:D], ACT.Copy).then_inc(setup_high, 1)
                act.activation(wv0T[:, 0, m, :], PS[:, 2 + m, 0:D], ACT.Copy).then_inc(setup_high, 1)
            act.wait_ge(w1_in, 16 * (3 + 2 * C))
            act.wait_ge(q_scaled, 2)
            for w in range(3):
                act.activation(w1[:, w, 0], w1in[:, w], ACT.Copy).then_inc(w1_high, 1)

            with act.Fori(0, B) as b:
                def fill_wait(name):
                    act.wait_ge(bank_filled, b * len(JOBS) + done(name))
                    return PS[:, bank(name)]

                def high_half(dst, name):
                    act.activation(dst, fill_wait(name), ACT.Copy).then_inc(high, 1)

                for q in range(2):
                    for c in range(C):
                        high_half(xT[:, 0, c, q * HALF:(q + 1) * HALF], ("xT", c, q))
                for m in range(C):
                    high_half(G[:, 0, m, :], ("G", 0, m))
                for p in range(T // 2):
                    high_half(v0h[:, 2 * p:2 * p + 2, :].rearrange("p t d -> p (t d)"), ("v0", p))

                def rel_high(h, tiles):
                    for m in tiles:
                        i = h * T + m
                        act.wait_ge(drained, 1 + b * len(JOBS) + done(("rel", h, m)))
                        act.activation(rel[:, 0, m, :], rf[:, i % 2], ACT.Copy).then_inc(high, 1)
                        if i >= 2:
                            act.wait_ge(sums_added, b * 2 * T + i - 1)
                        act.activation(sq[:, i % 2], rf[:, i % 2], ACT.Square).then_inc(squared, 1)

                def move_sums(h):
                    act.wait_ge(sums_added, b * 2 * T + (h + 1) * T)
                    if h:
                        act.wait_ge(cols_ready, b * 2 + h)
                    act.activation(sums, PS[:, SUMS], ACT.Copy).then_inc(sums_out, 1)

                def high_x1T(h):
                    for c in range(C):
                        high_half(x1T[h][0][:, c, :], ("x1T", h, c))

                def high_qk(h, parts):
                    for w in parts:
                        hg, q = divmod(w, 2)
                        dst = qhi[:, hg] if q else (k1 if hg else k0)[:, 0]
                        act.activation(dst[:, h * HALF:(h + 1) * HALF].bitcast(F32R), fill_wait(("qk", h, w)),
                                       ACT.Identity, bias=(bqc if q else bkc)[:, hg:hg + 1]).then_inc(high, 1)

                rel_high(0, range(T))
                for m in range(C):
                    high_half(G[:, 0, m, :], ("G", 1, m))
                move_sums(0)
                rel_high(1, range(TURN_AT))
                high_x1T(0)
                rel_high(1, range(TURN_AT, T))
                high_qk(0, (0,))
                move_sums(1)
                high_qk(0, (1,))
                high_qk(0, (2,))
                high_x1T(1)
                high_qk(1, (0, 1, 2))
                high_qk(0, (3,))

                def exps(u):
                    act.wait_ge(masked, b * UNITS + u + 1)
                    act.activation(nr[:, u % NRING], nr[:, u % NRING], ACT.Exp, bias=least[:, u:u + 1],
                                   scale=-1.0, accum_out=rowsum[:, u:u + 1]).then_inc(probs, 1)

                def rowsums_out(g):
                    act.wait_ge(rT_filled, 1 + b * GROUPS + g + 1)
                    act.wait_ge(o_ready, 1 + b * GROUPS + g)
                    act.activation(rT, PS[:, COLS, 0:GQ], ACT.Copy).then_inc(rT_ready, 1)

                exps(0)
                high_qk(1, (3,))
                exps(1)
                for u in range(UNITS):
                    g, r = divmod(u, UPG)
                    _, _, _, qi, j = unit(u)
                    if u == UPG + HPG - 1:
                        for head in range(HPG):
                            act.wait_ge(ks_in[1][head], (b + 1) * K_LOADS[1])
                    if r == 0 and g >= 2:
                        act.wait_ge(pv_done, 1 + b * GROUPS + g - 1)
                    act.wait_ge(turned_a, b * UNITS + u + 1)
                    act.activation(pt[:, g % 2, j, 0:TH, qi * P:(qi + 1) * P],
                                   PS[:, 4].rearrange("p (t q) -> p t q", q=P), ACT.Copy).then_inc(pt_a, 1)
                    if act_copies_second(u):
                        act.wait_ge(turned_b, b * UNITS + u + 1)
                        act.activation(pt[:, g % 2, j, TH:T, qi * P:(qi + 1) * P],
                                       PS[:, 5].rearrange("p (t q) -> p t q", q=P), ACT.Copy).then_inc(pt_b, 1)
                    if u + 2 < UNITS:
                        exps(u + 2)
                    if g >= 1 and r == 6:
                        rowsums_out(g - 1)
                rowsums_out(GROUPS - 1)

        @block.vector
        def _(dve):
            v = nc.vector
            for s in (drained, pt_b, o_ready, x1_ready, wo_drained):
                dve.sem_inc(s, 1)
            dve.sem_inc(out_done, 16)
            dve.wait_ge(w1_in, 16 * (3 + 2 * C))
            for what in (w1in[:, 0], bqc[:]):
                v.tensor_scalar(what, what, QSCALE, None, ALU.mult).then_inc(q_scaled, 1)
            v.memset(QS[PARTS * HD:P], 0.0).then_inc(stacks_ready, 1)
            v.memset(KS0[PARTS * HD:P], 0.0).then_inc(stacks_ready, 1)
            dve.wait_ge(setup_high, 2 * C)
            for m in range(C):
                v.tensor_tensor(A0[:, 1, m, :], PS[:, m, 0:D], A0[:, 0, m, :].bitcast(F32),
                                ALU.subtract).then_inc(setup_dve, 1)
                v.tensor_tensor(wv0T[:, 1, m, :], PS[:, 2 + m, 0:D], wv0T[:, 0, m, :].bitcast(F32),
                                ALU.subtract).then_inc(setup_dve, 1)
            dve.wait_ge(w1_high, 3)
            for w in range(3):
                v.tensor_tensor(w1[:, w, 1], w1in[:, w], w1[:, w, 0].bitcast(F32), ALU.subtract) \
                    .then_inc(w1_low, 1)
            dve.wait_ge(mask_in[0], 16)
            v.tensor_scalar(negmask[:, 0:TH], negmask[:, 0:TH], 1.0, -MASK, ALU.subtract, ALU.mult) \
                .then_inc(mask_ready, 1)

            with dve.Fori(0, B) as b:
                def fill_wait(name):
                    dve.wait_ge(bank_filled, b * len(JOBS) + done(name))
                    return PS[:, bank(name)]

                def low_half(dst, hi, name):
                    dve.wait_ge(high, b * len(CUT) + cut_high(name))
                    v.tensor_tensor(dst, PS[:, bank(name)], hi.bitcast(F32), ALU.subtract) \
                        .then_inc(drained, 1)

                for q in range(2):
                    for c in range(C):
                        cols = slice(q * HALF, (q + 1) * HALF)
                        low_half(xT[:, 1, c, cols], xT[:, 0, c, cols], ("xT", c, q))
                for m in range(C):
                    low_half(G[:, 1, m, :], G[:, 0, m, :], ("G", 0, m))
                for p in range(T // 2):
                    pair = [w[:, 2 * p:2 * p + 2, :].rearrange("p t d -> p (t d)") for w in v0]
                    low_half(pair[1], pair[0], ("v0", p))

                def low_x1T(h):
                    for c in range(C):
                        low_half(x1T[h][1][:, c, :], x1T[h][0][:, c, :], ("x1T", h, c))

                def mask_rel(h):
                    def cut_rel(m):
                        i = h * T + m
                        dve.wait_ge(high, b * len(CUT) + cut_high(("rel", h, m)))
                        v.tensor_tensor(rel[:, 1, m, :], rf[:, i % 2], rel[:, 0, m, :].bitcast(F32),
                                        ALU.subtract).then_inc(rel_cut, 1)

                    for m in range(T):
                        i = h * T + m
                        dve.wait_ge(adj_in[i % ADJ], (b * (2 * T // ADJ) + i // ADJ + 1) * 16)
                        if i >= 2:
                            dve.wait_ge(squared, b * 2 * T + i - 1)
                            dve.wait_ge(rel_cut, b * 2 * T + i - 1)
                        v.tensor_tensor(rf[:, i % 2], fill_wait(("rel", h, m)), adjr[:, i % ADJ], ALU.mult) \
                            .then_inc(drained, 1)
                        if m >= 1 and not (h == 1 and m == TURN_AT):
                            cut_rel(m - 1)
                        if h == 1 and m in (2, 3):
                            normalise([m])
                        if h == 1 and m == TURN_AT - 1:
                            cut_rel(m)
                            low_x1T(0)
                    cut_rel(T - 1)

                def norm_out(h):
                    dve.wait_ge(cols_ready, b * 2 + h + 1)
                    v.tensor_copy(nsq[:, h * TH:(h + 1) * TH], PS[:, COLS, 0:TH]).then_inc(nsq_ready, 1)

                def residual(h):
                    dve.wait_ge(rnorm_ready, b * 2 + h + 1)
                    if h == 0:
                        dve.wait_ge(out_done, 16 + b * 32)
                    for i in range(TH):
                        t = h * TH + i
                        v.scalar_tensor_tensor(out=x1[:, t], in0=fill_wait(("out", h, i))[:, 0:D],
                                               scalar=rnorm[:, t:t + 1], in1=xs[:, t], op0=ALU.mult,
                                               op1=ALU.add).then_inc(drained, 1)
                        dve.wait_ge(drained, 1 + b * len(JOBS) + done(("out", h, i)))
                        v.bn_stats(stats[:, t], x1[:, t]).then_inc(stat_step, 1)
                        if i == TH - 1 or (h == 1 and i == TH - 2):
                            alone(dve, stat_step, b * 2 * T + t + 1)
                            for n in range(h * TH, t + 1) if h == 0 or i < TH - 1 else (t,):
                                last = v.bn_aggr(mv[:, n], stats[:, n])
                            last.then_inc(var_ready, 1)

                def normalise(tiles):
                    dve.wait_ge(rstd_ready, b * 3 + (0, 1, 2)[(tiles[0] >= TH) + (tiles[0] == T - 1)] + 1)
                    for t in tiles:
                        v.tensor_scalar(x1[:, t], x1[:, t], mv[:, t, 0:1], rstd[:, t:t + 1],
                                        ALU.subtract, ALU.mult).then_inc(x1_ready, 1)

                def cut(h, parts):
                    for w in parts:
                        hg, q = divmod(w, 2)
                        cols = slice(h * HALF, (h + 1) * HALF)
                        kh = (k1 if hg else k0)
                        hi, lo = (qhi[:, hg], qlo[:, hg]) if q else (kh[:, 0], kh[:, 1])
                        dve.wait_ge(high, b * len(CUT) + cut_high(("qk", h, w)))
                        v.scalar_tensor_tensor(out=lo[:, cols].bitcast(F32R), in0=PS[:, bank(("qk", h, w))],
                                               scalar=(bqc if q else bkc)[:, hg:hg + 1], in1=hi[:, cols],
                                               op0=ALU.add, op1=ALU.subtract).then_inc(drained, 1)

                def add_bv(h, pairs):
                    if h == 0 and pairs[0] == 0:
                        dve.wait_ge(wo_in, 16 * 3)
                    for p in pairs:
                        t = h * TH + 2 * p
                        src = fill_wait(("v1", h, p)).rearrange("p (t d) -> p t d", d=D)
                        v.tensor_tensor(vs[:, t:t + 2, :], src, bvb[:].rearrange("p (a d) -> p a d", a=1)
                                        .to_broadcast([P, 2, D]), ALU.add).then_inc(drained, 1)

                mask_rel(0)
                for m in range(C):
                    low_half(G[:, 1, m, :], G[:, 0, m, :], ("G", 1, m))
                norm_out(0)
                residual(0)
                mask_rel(1)
                cut(0, (0, 1))
                norm_out(1)
                residual(1)
                normalise(range(TH, T - 1))
                normalise([T - 1])
                cut(0, (2,))
                add_bv(0, (0,))
                low_x1T(1)
                add_bv(0, (1,))
                cut(1, (0, 1))
                dve.wait_ge(mask_ready, 1 + TH)
                add_bv(1, (0, 1))

                def mask_scores(u):
                    _, _, q0, qi, _ = unit(u)
                    if u >= NRING:
                        dve.wait_ge(turned_b, b * UNITS + u - NRING + 1)
                    alone(dve, scores, 1 + b * UNITS + u + 1)
                    k = 2 * (u % 2)
                    v.tensor_tensor_reduce(out=nr[:, u % NRING], in0=PS[:, k:k + 2].rearrange("p k n -> p (k n)"),
                                           in1=negmask[:, q0 // P + qi], scale=1.0, scalar=3.0e38,
                                           op0=ALU.add, op1=ALU.min,
                                           accum_out=least[:, u:u + 1]).then_inc(masked, 1)

                def group_out(g):
                    _, hg, q0, _, _ = unit(g * UPG)
                    dve.wait_ge(pv_done, 1 + b * GROUPS + g + 1)
                    dve.wait_ge(rT_ready, 1 + b * GROUPS + g + 1)
                    v.tensor_tensor(QO[:, hg, q0:q0 + GQ], PS[:, out_bank(g), 0:GQ], rT, ALU.mult) \
                        .then_inc(o_ready, 1)

                def residual_out(p):
                    if p == 0:
                        dve.wait_ge(x1b_ready, (b + 1) * T)
                    dve.wait_ge(wo_filled, b * (T // 2) + p + 1)
                    dst = x1[:, 2 * p:2 * p + 2, :].rearrange("p t d -> p (t d)")
                    v.tensor_tensor(dst, PS[:, WO_BANK[p]], dst, ALU.add).then_inc(wo_drained, 1)

                def residual_var(p):
                    alone(dve, stat_step, b * 2 * T + T + 2 * p + 2)
                    for t in (2 * p, 2 * p + 1):
                        last = v.bn_aggr(mv[:, t], stats[:, t])
                    last.then_inc(var_ready, 1)

                def residual_stats(p, i):
                    dve.wait_ge(wo_drained, 1 + b * (T // 2) + p + 1)
                    v.bn_stats(stats[:, 2 * p + i], x1[:, 2 * p + i]).then_inc(stat_step, 1)

                cut(1, (2,))
                mask_scores(0)
                cut(0, (3,))
                mask_scores(1)
                for u in range(UNITS):
                    g, r = divmod(u, UPG)
                    _, _, _, qi, j = unit(u)
                    if r == 0 and g >= 2:
                        group_out(g - 2)
                    if u + 2 < UNITS:
                        mask_scores(u + 2)
                    if u == 2 * UPG - 1:
                        for head in range(HPG):
                            dve.wait_ge(ks_in[1][head], (b + 1) * K_LOADS[1])
                    if not act_copies_second(u):
                        dve.wait_ge(turned_b, b * UNITS + u + 1)
                        v.tensor_copy(pt[:, g % 2, j, TH:T, qi * P:(qi + 1) * P],
                                      PS[:, 5].rearrange("p (t q) -> p t q", q=P)).then_inc(pt_b, 1)
                    if u == 0:
                        cut(1, (3,))
                    if g == 6 and r == 2:
                        residual_out(0)
                    if g == 6 and r in (4, 5):
                        residual_stats(0, r - 4)
                    if g == 6 and r == 6:
                        residual_var(0)
                group_out(GROUPS - 2)
                residual_out(1)
                for i in range(2):
                    residual_stats(1, i)
                residual_var(1)
                group_out(GROUPS - 1)
                for p in (2, 3):
                    residual_out(p)
                    for i in range(2):
                        residual_stats(p, i)
                    residual_var(p)


_INS = ["x", "adj", "L0_gnn_Wq", "L0_gnn_Wk", "L0_gnn_Wv", "L1_gnn_Wq", "L1_gnn_bq", "L1_gnn_Wk", "L1_gnn_bk",
        "L1_gnn_Wv", "L1_gnn_bv", "L1_gnn_Wo", "L1_gnn_bo"]


def kernel(**inputs):
    import concourse.bacc as bacc
    from concourse.bass_utils import run_bass_kernel_spmd

    nc = bacc.Bacc("TRN2", target_bir_lowering=False, num_devices=1, dynamic_dma_scratch_size=2048)
    arrays, args = {}, []
    for name in _INS:
        a = np.ascontiguousarray(inputs[name])
        arrays[f"in_{name}"] = a
        args.append(nc.dram_tensor(f"in_{name}", a.shape, mybir.dt.from_np(a.dtype), kind="ExternalInput").ap())
    out = nc.dram_tensor("out_0", (B, N, D), F32, kind="ExternalOutput").ap()
    build(nc, *args, out)
    r = run_bass_kernel_spmd(nc, [arrays], core_ids=[0])
    return r.results[0]["out_0"]
```
